# Optimizing a Trainium2 kernel written in Bass

```python
import numpy as np
import jax
import jax.numpy as jnp

def _softmax(x, axis=-1):
    return jax.nn.softmax(x, axis=axis)

def _gelu(x):
    return jax.nn.gelu(x, approximate=True)

def _silu(x):
    return jax.nn.silu(x)

def _sigmoid(x):
    return jax.nn.sigmoid(x)

def _layernorm(x, axis=-1, eps=1e-05):
    m = jnp.mean(x, axis=axis, keepdims=True)
    v = jnp.var(x, axis=axis, keepdims=True)
    return (x - m) / jnp.sqrt(v + eps)

def _scatter_add(tgt, idx, src, axis=0):
    return tgt.at[idx].add(src)

def _segment_sum(src, seg, n):
    return jax.ops.segment_sum(src, seg, n)
kernel_name = 'mk_xattn_seq_d2_seqx_r8_737aa5'

def setup_inputs(seed: int=0):
    np.random.seed(seed)
    _w = jnp.asarray

    def _rec_inputs():
        import jax
        import jax.numpy as jnp
        _rk = jax.random.key(seed)
        x = 7.22e-05 + 1 * jax.random.normal(jax.random.fold_in(_rk, 1), (16, 128, 256), jnp.float32)
        _lenS = 128 - jax.random.randint(jax.random.fold_in(_rk, 7), (16,), 0, max(1, 128 // 4) + 1, jnp.int32)
        _lenS2 = 128 - jax.random.randint(jax.random.fold_in(_rk, 8), (16,), 0, max(1, 128 // 4) + 1, jnp.int32)
        _ctx_2048P = jax.random.normal(jax.random.fold_in(_rk, 11), (16, 16, 256), jnp.float32)
        _ctx_2048c = jax.random.dirichlet(jax.random.fold_in(_rk, 511), 0.3 * jnp.ones((16,), jnp.float32), (16, 128))
        _ctx_2048t = jnp.einsum('bsk,bkd->bsd', _ctx_2048c, _ctx_2048P)
        _ctx_2048t = _ctx_2048t * jax.lax.rsqrt(jnp.mean(jnp.square(_ctx_2048t)) + 1e-12) * 0.953939
        ctx_2048 = 4.13588e-05 + 0.999923 * (_ctx_2048t + 0.3 * jax.random.normal(jax.random.fold_in(_rk, 611), (16, 128, 256), jnp.float32))
        _validS = jnp.arange(128)[None, :] < _lenS[:, None]
        _validS2 = jnp.arange(128)[None, :] < _lenS2[:, None]
        _causal = jnp.tril(jnp.ones((128, 128), dtype=bool))
        mask_Bx1xSxS2_ff0 = jnp.where(jnp.ones((16, 1, 128, 128), dtype=bool), 0.0, -1000000000.0).astype(jnp.float32)
        return (x, ctx_2048, mask_Bx1xSxS2_ff0)
    x, ctx_2048, mask_Bx1xSxS2_ff0 = _rec_inputs()

    def _L0_xattn_setup():
        import jax, jax.numpy as jnp
        import numpy as np
        H = 256
        NH = 32
        KVH = 8
        HD = H // NH
        GROUPS = NH // KVH
        EPS = 1e-06
        B, L, S = (4, 128, 128)

        def _gqa_forward(hidden_state, encoder_hidden_state, encoder_attention_mask, Wq, bq, Wk, bk, Wv, bv, Wo, bo, gamma, beta):
            b, l, _ = hidden_state.shape
            s = encoder_hidden_state.shape[1]
            q = hidden_state @ Wq + bq
            k = encoder_hidden_state @ Wk + bk
            v = encoder_hidden_state @ Wv + bv
            q = q.reshape(b, l, KVH, GROUPS, HD).transpose(0, 2, 3, 1, 4)
            k = k.reshape(b, s, KVH, HD).transpose(0, 2, 1, 3)
            v = v.reshape(b, s, KVH, HD).transpose(0, 2, 1, 3)
            scale = 1.0 / jnp.sqrt(jnp.asarray(HD, q.dtype))
            scores = jnp.einsum('bkgld,bksd->bkgls', q, k) * scale
            scores = scores + encoder_attention_mask[:, :, None, :, :]
            attn = jax.nn.softmax(scores, axis=-1)
            out = jnp.einsum('bkgls,bksd->bkgld', attn, v)
            out = out.transpose(0, 3, 1, 2, 4).reshape(b, l, H)
            out = out @ Wo + bo
            x = out + hidden_state
            mu = jnp.mean(x, axis=-1, keepdims=True)
            var = jnp.var(x, axis=-1, keepdims=True)
            return (x - mu) * jax.lax.rsqrt(var + EPS) * gamma + beta
        key = jax.random.key(seed)
        ks = jax.random.split(key, 12)
        sd = 0.02
        return {'hidden_state': jax.random.normal(ks[0], (B, L, H), jnp.float32), 'encoder_hidden_state': jax.random.normal(ks[1], (B, S, H), jnp.float32), 'encoder_attention_mask': jnp.zeros((B, 1, L, S), jnp.float32), 'Wq': jax.random.normal(ks[2], (H, H), jnp.float32) * sd, 'bq': jnp.zeros((H,), jnp.float32), 'Wk': jax.random.normal(ks[3], (H, KVH * HD), jnp.float32) * sd, 'bk': jnp.zeros((KVH * HD,), jnp.float32), 'Wv': jax.random.normal(ks[4], (H, KVH * HD), jnp.float32) * sd, 'bv': jnp.zeros((KVH * HD,), jnp.float32), 'Wo': jax.random.normal(ks[5], (H, H), jnp.float32) * sd, 'bo': jnp.zeros((H,), jnp.float32), 'gamma': jnp.ones((H,), jnp.float32), 'beta': jnp.zeros((H,), jnp.float32)}
    _L0_xattn_all = _L0_xattn_setup()
    _L0_xattn_in = {k: v for k, v in _L0_xattn_all.items() if k in ('Wq', 'bq', 'Wk', 'bk', 'Wv', 'bv', 'Wo', 'bo', 'gamma', 'beta')}
    del _L0_xattn_all

    def _L1_xattn_setup():
        import jax, jax.numpy as jnp
        import numpy as np
        H = 256
        NH = 32
        KVH = 8
        HD = H // NH
        GROUPS = NH // KVH
        EPS = 1e-06
        B, L, S = (4, 128, 128)

        def _gqa_forward(hidden_state, encoder_hidden_state, encoder_attention_mask, Wq, bq, Wk, bk, Wv, bv, Wo, bo, gamma, beta):
            b, l, _ = hidden_state.shape
            s = encoder_hidden_state.shape[1]
            q = hidden_state @ Wq + bq
            k = encoder_hidden_state @ Wk + bk
            v = encoder_hidden_state @ Wv + bv
            q = q.reshape(b, l, KVH, GROUPS, HD).transpose(0, 2, 3, 1, 4)
            k = k.reshape(b, s, KVH, HD).transpose(0, 2, 1, 3)
            v = v.reshape(b, s, KVH, HD).transpose(0, 2, 1, 3)
            scale = 1.0 / jnp.sqrt(jnp.asarray(HD, q.dtype))
            scores = jnp.einsum('bkgld,bksd->bkgls', q, k) * scale
            scores = scores + encoder_attention_mask[:, :, None, :, :]
            attn = jax.nn.softmax(scores, axis=-1)
            out = jnp.einsum('bkgls,bksd->bkgld', attn, v)
            out = out.transpose(0, 3, 1, 2, 4).reshape(b, l, H)
            out = out @ Wo + bo
            x = out + hidden_state
            mu = jnp.mean(x, axis=-1, keepdims=True)
            var = jnp.var(x, axis=-1, keepdims=True)
            return (x - mu) * jax.lax.rsqrt(var + EPS) * gamma + beta
        key = jax.random.key(seed)
        ks = jax.random.split(key, 12)
        sd = 0.02
        return {'hidden_state': jax.random.normal(ks[0], (B, L, H), jnp.float32), 'encoder_hidden_state': jax.random.normal(ks[1], (B, S, H), jnp.float32), 'encoder_attention_mask': jnp.zeros((B, 1, L, S), jnp.float32), 'Wq': jax.random.normal(ks[2], (H, H), jnp.float32) * sd, 'bq': jnp.zeros((H,), jnp.float32), 'Wk': jax.random.normal(ks[3], (H, KVH * HD), jnp.float32) * sd, 'bk': jnp.zeros((KVH * HD,), jnp.float32), 'Wv': jax.random.normal(ks[4], (H, KVH * HD), jnp.float32) * sd, 'bv': jnp.zeros((KVH * HD,), jnp.float32), 'Wo': jax.random.normal(ks[5], (H, H), jnp.float32) * sd, 'bo': jnp.zeros((H,), jnp.float32), 'gamma': jnp.ones((H,), jnp.float32), 'beta': jnp.zeros((H,), jnp.float32)}
    _L1_xattn_all = _L1_xattn_setup()
    _L1_xattn_in = {k: v for k, v in _L1_xattn_all.items() if k in ('Wq', 'bq', 'Wk', 'bk', 'Wv', 'bv', 'Wo', 'bo', 'gamma', 'beta')}
    del _L1_xattn_all
    return {'x': x, 'ctx_2048': ctx_2048, 'mask_Bx1xSxS2_ff0': mask_Bx1xSxS2_ff0, 'L0_xattn_Wq': _L0_xattn_in['Wq'], 'L0_xattn_bq': _L0_xattn_in['bq'], 'L0_xattn_Wk': _L0_xattn_in['Wk'], 'L0_xattn_bk': _L0_xattn_in['bk'], 'L0_xattn_Wv': _L0_xattn_in['Wv'], 'L0_xattn_bv': _L0_xattn_in['bv'], 'L0_xattn_Wo': _L0_xattn_in['Wo'], 'L0_xattn_bo': _L0_xattn_in['bo'], 'L0_xattn_gamma': _L0_xattn_in['gamma'], 'L0_xattn_beta': _L0_xattn_in['beta'], 'L1_xattn_Wq': _L1_xattn_in['Wq'], 'L1_xattn_bq': _L1_xattn_in['bq'], 'L1_xattn_Wk': _L1_xattn_in['Wk'], 'L1_xattn_bk': _L1_xattn_in['bk'], 'L1_xattn_Wv': _L1_xattn_in['Wv'], 'L1_xattn_bv': _L1_xattn_in['bv'], 'L1_xattn_Wo': _L1_xattn_in['Wo'], 'L1_xattn_bo': _L1_xattn_in['bo'], 'L1_xattn_gamma': _L1_xattn_in['gamma'], 'L1_xattn_beta': _L1_xattn_in['beta']}

def reference(x, ctx_2048, mask_Bx1xSxS2_ff0, L0_xattn_Wq, L0_xattn_bq, L0_xattn_Wk, L0_xattn_bk, L0_xattn_Wv, L0_xattn_bv, L0_xattn_Wo, L0_xattn_bo, L0_xattn_gamma, L0_xattn_beta, L1_xattn_Wq, L1_xattn_bq, L1_xattn_Wk, L1_xattn_bk, L1_xattn_Wv, L1_xattn_bv, L1_xattn_Wo, L1_xattn_bo, L1_xattn_gamma, L1_xattn_beta):
    import jax
    import jax.numpy as jnp

    def _L0_xattn_ref(hidden_state, encoder_hidden_state, encoder_attention_mask, Wq, bq, Wk, bk, Wv, bv, Wo, bo, gamma, beta):
        import jax, jax.numpy as jnp
        import numpy as np
        H = 256
        NH = 32
        KVH = 8
        HD = H // NH
        GROUPS = NH // KVH
        EPS = 1e-06
        B, L, S = (4, 128, 128)

        def _gqa_forward(hidden_state, encoder_hidden_state, encoder_attention_mask, Wq, bq, Wk, bk, Wv, bv, Wo, bo, gamma, beta):
            b, l, _ = hidden_state.shape
            s = encoder_hidden_state.shape[1]
            q = hidden_state @ Wq + bq
            k = encoder_hidden_state @ Wk + bk
            v = encoder_hidden_state @ Wv + bv
            q = q.reshape(b, l, KVH, GROUPS, HD).transpose(0, 2, 3, 1, 4)
            k = k.reshape(b, s, KVH, HD).transpose(0, 2, 1, 3)
            v = v.reshape(b, s, KVH, HD).transpose(0, 2, 1, 3)
            scale = 1.0 / jnp.sqrt(jnp.asarray(HD, q.dtype))
            scores = jnp.einsum('bkgld,bksd->bkgls', q, k) * scale
            scores = scores + encoder_attention_mask[:, :, None, :, :]
            attn = jax.nn.softmax(scores, axis=-1)
            out = jnp.einsum('bkgls,bksd->bkgld', attn, v)
            out = out.transpose(0, 3, 1, 2, 4).reshape(b, l, H)
            out = out @ Wo + bo
            x = out + hidden_state
            mu = jnp.mean(x, axis=-1, keepdims=True)
            var = jnp.var(x, axis=-1, keepdims=True)
            return (x - mu) * jax.lax.rsqrt(var + EPS) * gamma + beta
        return _gqa_forward(hidden_state, encoder_hidden_state, encoder_attention_mask, Wq, bq, Wk, bk, Wv, bv, Wo, bo, gamma, beta)

    def _L1_xattn_ref(hidden_state, encoder_hidden_state, encoder_attention_mask, Wq, bq, Wk, bk, Wv, bv, Wo, bo, gamma, beta):
        import jax, jax.numpy as jnp
        import numpy as np
        H = 256
        NH = 32
        KVH = 8
        HD = H // NH
        GROUPS = NH // KVH
        EPS = 1e-06
        B, L, S = (4, 128, 128)

        def _gqa_forward(hidden_state, encoder_hidden_state, encoder_attention_mask, Wq, bq, Wk, bk, Wv, bv, Wo, bo, gamma, beta):
            b, l, _ = hidden_state.shape
            s = encoder_hidden_state.shape[1]
            q = hidden_state @ Wq + bq
            k = encoder_hidden_state @ Wk + bk
            v = encoder_hidden_state @ Wv + bv
            q = q.reshape(b, l, KVH, GROUPS, HD).transpose(0, 2, 3, 1, 4)
            k = k.reshape(b, s, KVH, HD).transpose(0, 2, 1, 3)
            v = v.reshape(b, s, KVH, HD).transpose(0, 2, 1, 3)
            scale = 1.0 / jnp.sqrt(jnp.asarray(HD, q.dtype))
            scores = jnp.einsum('bkgld,bksd->bkgls', q, k) * scale
            scores = scores + encoder_attention_mask[:, :, None, :, :]
            attn = jax.nn.softmax(scores, axis=-1)
            out = jnp.einsum('bkgls,bksd->bkgld', attn, v)
            out = out.transpose(0, 3, 1, 2, 4).reshape(b, l, H)
            out = out @ Wo + bo
            x = out + hidden_state
            mu = jnp.mean(x, axis=-1, keepdims=True)
            var = jnp.var(x, axis=-1, keepdims=True)
            return (x - mu) * jax.lax.rsqrt(var + EPS) * gamma + beta
        return _gqa_forward(hidden_state, encoder_hidden_state, encoder_attention_mask, Wq, bq, Wk, bk, Wv, bv, Wo, bo, gamma, beta)
    x = _L0_xattn_ref(x, ctx_2048, mask_Bx1xSxS2_ff0, L0_xattn_Wq, L0_xattn_bq, L0_xattn_Wk, L0_xattn_bk, L0_xattn_Wv, L0_xattn_bv, L0_xattn_Wo, L0_xattn_bo, L0_xattn_gamma, L0_xattn_beta)
    x = _L1_xattn_ref(x, ctx_2048, mask_Bx1xSxS2_ff0, L1_xattn_Wq, L1_xattn_bq, L1_xattn_Wk, L1_xattn_bk, L1_xattn_Wv, L1_xattn_bv, L1_xattn_Wo, L1_xattn_bo, L1_xattn_gamma, L1_xattn_beta)
    return x

_drawn_inputs = setup_inputs


def setup_inputs(seed=0):
    import zlib

    import numpy as np

    out = dict(_drawn_inputs(seed))
    spreads = {'L0_xattn_bq': (0.0, 0.8),
     'L0_xattn_bk': (0.0, 0.8),
     'L0_xattn_bv': (0.0, 0.1),
     'L0_xattn_bo': (0.0, 0.1),
     'L0_xattn_gamma': (1.0, 0.2),
     'L0_xattn_beta': (0.0, 0.1),
     'L1_xattn_bq': (0.0, 0.8),
     'L1_xattn_bk': (0.0, 0.8),
     'L1_xattn_bv': (0.0, 0.1),
     'L1_xattn_bo': (0.0, 0.1),
     'L1_xattn_gamma': (1.0, 0.2),
     'L1_xattn_beta': (0.0, 0.1)}
    factors = {'L0_xattn_Wq': 8.0, 'L0_xattn_Wk': 8.0, 'L1_xattn_Wq': 8.0, 'L1_xattn_Wk': 8.0}
    for name, (base, spread) in spreads.items():
        noise = np.random.default_rng([zlib.crc32(name.encode()), seed]).standard_normal(out[name].shape)
        drawn = base * np.exp(spread * noise) if base else spread * noise
        out[name] = jnp.asarray(drawn.astype(out[name].dtype))
    for name, factor in factors.items():
        out[name] = (out[name] * factor).astype(out[name].dtype)
    return out
```

```python
from contextlib import ExitStack

import concourse.bass as bass
import numpy as np
from concourse import mybir

F32 = mybir.dt.float32
BF16 = mybir.dt.bfloat16
I32 = mybir.dt.int32
ALU = mybir.AluOpType
ACT = mybir.ActivationFunctionType
AX = mybir.AxisListType

P = 128
LAYERS, BATCH, L, S, D = 2, 16, 128, 128, 256
HEADS, KV, HD = 32, 8, 8
GROUP = HEADS // KV
KT = D // P
UNITS = LAYERS * BATCH
PARTS = 3
TERM_ROWS = PARTS * PARTS * HD
SCORE_ROWS = 96
MAX_ROW = 96
STACK_ROWS = MAX_ROW + PARTS
RING = 4
HALF = KV // 2
KVD = KV * HD
SCALE = float(HD) ** -0.5
EPS = 1e-6
LOOP_FROM, LOOP_TO = 4, 28
FIRST_PHASE, LAST_PHASE = -2, UNITS + 2


def live(u):
    return not isinstance(u, int) or 0 <= u < UNITS


def need(engine, sem, count):
    if not isinstance(count, int) or count > 0:
        engine.wait_ge(sem, count)


def upto(u):
    return min(u, UNITS - 1) if isinstance(u, int) else u


def walk(engine, phase):
    for t in range(FIRST_PHASE, LOOP_FROM):
        phase(t, t % RING)
    with engine.Fori(LOOP_FROM, LOOP_TO - RING + 1, RING) as turn:
        for r in range(RING):
            phase(turn + r, r)
    for t in range(LOOP_TO, LAST_PHASE + 1):
        phase(t, t % RING)


def cross_attention(nc, x, xT, ctxT, mask, w_qkv, w_o, b_q, b_k, rows, out):
    with ExitStack() as ctx:
        def sb(name, shape, dt):
            return ctx.enter_context(nc.sbuf_tensor(name, shape, dt))

        def sem(name):
            return ctx.enter_context(nc.semaphore(name))

        q_scratch = nc.dram_tensor("q_scratch", (UNITS, PARTS, P, KT * L), BF16).ap()
        k_scratch = nc.dram_tensor("k_scratch", (UNITS, PARTS, KVD, S), BF16).ap()

        x_sb = sb("x_sb", [P, BATCH, D], F32)
        xT_sb = sb("xT_sb", [P, KT, BATCH, L], F32)
        ctx_sb = sb("ctx_sb", [P, RING, KT, S], F32)
        mask_sb = sb("mask_sb", [P, BATCH, S], F32)
        mask_parts = sb("mask_parts", [P, RING, PARTS, S], BF16)
        w_now = sb("w_now", [P, KT, D + 2 * KVD], F32)
        wo_sb = sb("wo_sb", [P, LAYERS, KT, D], F32)
        bq_sb = sb("bq_sb", [P, LAYERS, KT], F32)
        bq_scaled = sb("bq_scaled", [P, LAYERS, KT], F32)
        bk_sb = sb("bk_sb", [KVD, LAYERS], F32)
        rows_sb = sb("rows_sb", [P, LAYERS, 3 * D + KVD], F32)
        identf = sb("identf", [P, P], F32)
        ident = sb("ident", [P, P], BF16)
        qT = sb("qT", [P, KT * L], F32)
        kT = sb("kT", [KVD, S], F32)
        q_rest = sb("q_rest", [P, KT * L], F32)
        k_rest = sb("k_rest", [KVD, S], F32)
        mask_now = sb("mask_now", [P, 2, S], F32)
        zeros = sb("zeros", [P, S], F32)
        held = sb("held", [P, 3], F32)
        held_v = sb("held_v", [P, 1], F32)
        m_rest = sb("m_rest", [P, S], F32)
        q_parts = sb("q_parts", [P, 2, PARTS, KT * L], BF16)
        k_parts = sb("k_parts", [KVD, 2, PARTS, S], BF16)
        q_stack = sb("q_stack", [P, RING, HEADS, L], BF16)
        k_stack = sb("k_stack", [P, RING, KV, S], BF16)
        row_max = sb("row_max", [P, 2, HEADS], F32)
        max_rest = sb("max_rest", [HEADS, L], F32)
        max_parts = sb("max_parts", [HEADS, 2, PARTS, L], BF16)
        v_ones = sb("v_ones", [P, RING, KV, 32], F32)
        probs = sb("probs", [P, 2, KV, GROUP * L], F32)
        oT_sb = sb("oT_sb", [P, 2, GROUP * L], F32)
        recip = sb("recip", [P, 2, 16], F32)
        attn = sb("attn", [P, D], F32)
        attnT = sb("attnT", [P, KT, L], F32)
        x_bo = sb("x_bo", [P, D], F32)
        z = sb("z", [P, D], F32)
        stats = sb("stats", [P, 6], F32)
        mean_var = sb("mean_var", [P, 2], F32)
        var_eps = sb("var_eps", [P, 1], F32)
        minus_half = sb("minus_half", [P, 1], F32)
        rstd = sb("rstd", [P, 1], F32)
        normed = sb("normed", [P, D], F32)
        scaled = sb("scaled", [P, D], F32)
        y = sb("y", [P, 2, D], F32)
        mask_top = sb("mask_top", [P, 1], F32)
        mask_any = sb("mask_any", [P, 1], F32)
        mask_flag = sb("mask_flag", [P, 1], I32)

        def bank(name):
            return ctx.enter_context(nc.psum_tensor(name, [P, 512], F32))

        s_bank = [bank("s_bank0"), bank("s_bank1")]
        t_bank = [bank("t_bank0"), bank("t_bank1")]
        oT_bank = bank("oT_bank")
        o_bank = bank("o_bank")
        qk_bank = bank("qk_bank")
        misc_bank = bank("misc_bank")

        w_loaded = sem("w_loaded")
        consts_loaded = sem("consts_loaded")
        xT_loaded = sem("xT_loaded")
        x_loaded = sem("x_loaded")
        mask_loaded = sem("mask_loaded")
        all_masks_loaded = sem("all_masks_loaded")
        ctx_loaded = sem("ctx_loaded")
        ident_step = sem("ident_step")
        pad_step = sem("pad_step")
        padded = sem("padded")
        bias_scaled = sem("bias_scaled")
        flag_step = sem("flag_step")
        flag_ready = sem("flag_ready")
        mask_step = sem("mask_step")
        qk_projected = sem("qk_projected")
        v_projected = sem("v_projected")
        qk_read = sem("qk_read")
        v_ready = sem("v_ready")
        split_step = sem("split_step")
        parts_stored = sem("parts_stored")
        stacks_loaded = sem("stacks_loaded")
        scores_ready = sem("scores_ready")
        max_done = sem("max_done")
        maxT_ready = sem("maxT_ready")
        maxT_step = sem("maxT_step")
        max_rows_loaded = sem("max_rows_loaded")
        scoresT_ready = sem("scoresT_ready")
        exp_done = sem("exp_done")
        oT_ready = sem("oT_ready")
        oT_copied = sem("oT_copied")
        o_ready = sem("o_ready")
        recip_done = sem("recip_done")
        o_normed = sem("o_normed")
        attnT_ready = sem("attnT_ready")
        attnT_copied = sem("attnT_copied")
        proj_ready = sem("proj_ready")
        x_bo_ready = sem("x_bo_ready")
        rstd_ready = sem("rstd_ready")
        norm_step = sem("norm_step")
        affine_step = sem("affine_step")
        yT_ready = sem("yT_ready")
        yT_copied = sem("yT_copied")
        y_left = sem("y_left")

        MAXT_STEPS, NORM_STEPS = 4, 5
        SPLIT_STEPS = 6
        QK_READS = 6
        STACK_DMAS, MAX_ROW_DMAS = 6, 3
        CONST_DMAS = 4
        block = ctx.enter_context(nc.Block())

        @block.sync
        def _(sp):
            def load_weights(layer):
                sp.dma_start(w_now[:], w_qkv[layer].rearrange("(k p) n -> p k n", p=P)).then_inc(w_loaded, 16)

            def load_context(u, r):
                b = u % BATCH
                sp.dma_start(ctx_sb[:, r], ctxT[b].rearrange("(k p) s -> p k s", p=P)).then_inc(ctx_loaded, 16)

            load_weights(0)
            load_context(0, 0)
            sp.dma_start(xT_sb[:], xT.rearrange("(k p) b l -> p k b l", p=P)).then_inc(xT_loaded, 16)
            sp.dma_start(bq_sb[:], b_q).then_inc(consts_loaded, 16)
            sp.dma_start(bk_sb[:], b_k).then_inc(consts_loaded, 16)
            sp.dma_start(rows_sb[:].rearrange("p a n -> p (a n)"), rows.partition_broadcast(P)).then_inc(consts_loaded, 16)
            sp.dma_start(mask_sb[:], mask.rearrange("b o l s -> l (b o) s")).then_inc(all_masks_loaded, 16)
            sp.dma_start(wo_sb[:], w_o.rearrange("a (k p) n -> p a k n", p=P)).then_inc(consts_loaded, 16)
            sp.dma_start(x_sb[:], x.rearrange("b l d -> l b d")).then_inc(x_loaded, 16)

            def phase(turn, step, last_layer):
                t, r = turn + step, step % RING

                def of(per, k):
                    return turn * per + per * (step + k)

                if not isinstance(turn, int):
                    for per, k in ((16, 3), (4, 0), (16 * STACK_DMAS, 2), (SPLIT_STEPS, 3), (2, -2), (16, -3),
                                   (32, 3), (KV, 3 - RING), (MAXT_STEPS, 1), (16 * MAX_ROW_DMAS, 0), (KV, 1 - RING), (1, -2), (1, 0)):
                        sp.to_reg(of(per, k))
                if live(t + 3):
                    need(sp, qk_projected, of(1, 0))
                    need(sp, v_projected, of(1, 0))
                    need(sp, ctx_loaded, of(16, 3))
                    load_context(t + 3, (r + 3) % RING)
                u, ru = t + 1, (r + 1) % RING
                if live(u):
                    need(sp, mask_step, of(4, 0))
                    sp.dma_start(mask_now[:, ru % 2], mask[u % BATCH, 0]).then_inc(mask_loaded, 16)
                if live(t):
                    need(sp, maxT_step, of(MAXT_STEPS, 1))
                    need(sp, max_rows_loaded, of(16 * MAX_ROW_DMAS, 0))
                    need(sp, scoresT_ready, of(KV, 1 - RING))
                    for part in range(PARTS):
                        row = MAX_ROW + part
                        sp.dma_start(q_stack[row:row + 1, r], max_parts[:, r % 2, part]).then_inc(max_rows_loaded, 16)
                u, ru = t + 2, (r + 2) % RING
                if live(u):
                    need(sp, stacks_loaded, of(16 * STACK_DMAS, 2))
                    need(sp, split_step, of(SPLIT_STEPS, 3))
                    sp.dma_start(q_scratch[u].rearrange("a p n -> p a n"), q_parts[:, ru % 2]).then_inc(parts_stored, 16)
                    sp.dma_start(k_scratch[u].rearrange("a p n -> p a n"), k_parts[:, ru % 2]).then_inc(parts_stored, 16)
                    if isinstance(u, int) and u == BATCH - 1:
                        need(sp, v_projected, BATCH)
                        need(sp, qk_projected, BATCH)
                        load_weights(1)
                u, ru = t - 3, (r - 3) % RING
                if live(u):
                    b = u % BATCH
                    need(sp, affine_step, of(2, -2))
                    need(sp, y_left, of(16, -3))
                    if last_layer:
                        sp.dma_start(out[b], y[:, ru % 2]).then_inc(y_left, 16)
                    else:
                        need(sp, x_bo_ready, of(1, -2))
                        sp.dma_start(x_sb[:, b], y[:, ru % 2]).then_inc(y_left, 16)
                u, ru = t + 2, (r + 2) % RING
                if live(u):
                    need(sp, parts_stored, of(32, 3))
                    need(sp, scoresT_ready, of(KV, 3 - RING))
                    if isinstance(u, int) and u < RING:
                        need(sp, padded, 1)
                    q_rows = q_scratch[u].rearrange("a (d h) n -> (a d) (h n)", d=HD)
                    for part in range(PARTS):
                        first = part * PARTS * HD
                        sp.dma_start(q_stack[first:first + PARTS * HD, ru].rearrange("p h l -> p (h l)"),
                                     q_rows).then_inc(stacks_loaded, 16)
                        k_rows = k_scratch[u, part].rearrange("(d h) n -> d (h n)", d=HD)
                        sp.dma_start(k_stack[first:first + PARTS * HD, ru].rearrange("p h l -> p (h l)"),
                                     k_rows.partition_broadcast(PARTS)).then_inc(stacks_loaded, 16)

            change = BATCH + 3
            middle = change // RING * RING
            for t in range(FIRST_PHASE, LOOP_FROM):
                phase(0, t, False)
            with sp.Fori(LOOP_FROM, middle - 2 * RING + 1, RING) as turn:
                for r in range(RING):
                    phase(turn, r, False)
            for t in range(middle - RING, middle + RING):
                phase(0, t, t >= change)
            with sp.Fori(middle + RING, LOOP_TO - RING + 1, RING) as turn:
                for r in range(RING):
                    phase(turn, r, True)
            for t in range(LOOP_TO, LAST_PHASE + 1):
                phase(0, t, True)
            sp.wait_ge(y_left, 16 * UNITS)
            sp.wait_ge(parts_stored, 32 * UNITS)

        @block.gpsimd
        def _(pool):
            nc.gpsimd.memset(identf[:], 0.0).then_inc(ident_step, 1)
            nc.gpsimd.memset(ident[:], 0.0).then_inc(ident_step, 1)
            pool.wait_ge(ident_step, 2)
            nc.gpsimd.memset(zeros[:], 0.0).then_inc(ident_step, 1)
            nc.gpsimd.memset(minus_half[:], -0.5).then_inc(ident_step, 1)
            for m in (identf, ident):
                nc.gpsimd.affine_select(out=m[:], in_=m[:], compare_op=ALU.not_equal, fill=1.0, base=0,
                                        pattern=[[-1, P]], channel_multiplier=1).then_inc(ident_step, 1)

            def flags():
                pool.wait_ge(flag_step, 1)
                nc.gpsimd.partition_all_reduce(mask_any[:], mask_top[:], P, bass.bass_isa.ReduceOp.max).then_inc(flag_step, 1)

            def split(f, rest, parts, step, done):
                nc.gpsimd.tensor_tensor(rest, f, parts[0], ALU.subtract).then_inc(step, 1)
                nc.gpsimd.tensor_tensor(parts[1], f, parts[0], ALU.subtract).then_inc(step, 1)
                pool.wait_ge(step, done + 2)
                nc.gpsimd.tensor_tensor(parts[2], rest, parts[1], ALU.subtract).then_inc(step, 1)

            def hold(n):
                nc.gpsimd.tensor_tensor(held[:, n:n + 1], minus_half[:], minus_half[:], ALU.add)

            def phase(t, r):
                u = t - 3
                if live(u):
                    layer = u // BATCH
                    need(pool, norm_step, NORM_STEPS * u + 4)
                    nc.gpsimd.tensor_tensor(rstd[:], var_eps[:], minus_half[:], ALU.pow).then_inc(rstd_ready, 1)
                    need(pool, norm_step, NORM_STEPS * (u + 1))
                    need(pool, affine_step, 2 * u)
                    hold(0)
                    nc.gpsimd.tensor_tensor(scaled[:], normed[:], rows_sb[:, layer, D:2 * D],
                                            ALU.mult).then_inc(affine_step, 1)
                    need(pool, yT_ready, u - 1)
                    need(pool, y_left, 16 * (u - 1))
                    pool.wait_ge(affine_step, 2 * u + 1)
                    hold(1)
                    nc.gpsimd.tensor_tensor(y[:, (r - 3) % 2], scaled[:], rows_sb[:, layer, 2 * D:3 * D],
                                            ALU.add).then_inc(affine_step, 1)
                u, ru = t + 2, (r + 2) % RING
                if live(u):
                    need(pool, qk_read, QK_READS * (u + 1))
                    split(qT[:], q_rest[:], [q_parts[:, ru % 2, n] for n in range(PARTS)], split_step, SPLIT_STEPS * u)
                    split(kT[:], k_rest[:], [k_parts[:, ru % 2, n] for n in range(PARTS)], split_step,
                          SPLIT_STEPS * u + 3)
                u, ru = t + 1, (r + 1) % RING
                if live(u):
                    need(pool, mask_loaded, 16 * (u + 1))
                    need(pool, scoresT_ready, KV * (u - RING + 1))
                    parts = [mask_parts[:, ru, n] for n in range(PARTS)]
                    nc.gpsimd.tensor_tensor(parts[0], mask_now[:, ru % 2], zeros[:], ALU.add).then_inc(mask_step, 1)
                    pool.wait_ge(mask_step, 4 * u + 1)
                    split(mask_now[:, ru % 2], m_rest[:], parts, mask_step, 4 * u + 1)
                u = t - 2
                if live(u):
                    if isinstance(u, int) and u == 0:
                        pool.wait_ge(x_loaded, 16)
                        pool.wait_ge(consts_loaded, 16 * CONST_DMAS)
                    need(pool, norm_step, NORM_STEPS * (u - 1) + 1)
                    hold(2)
                    nc.gpsimd.tensor_tensor(x_bo[:], x_sb[:, u % BATCH], rows_sb[:, u // BATCH, 0:D],
                                            ALU.add).then_inc(x_bo_ready, 1)

            pool.wait_ge(ident_step, 6)
            flags()
            walk(pool, phase)

        @block.scalar
        def _(act):
            def exp(u, ru, kv):
                need(act, scoresT_ready, KV * u + kv + 1)
                need(act, oT_ready, 2 * (u - 2) + kv // HALF + 1)
                nc.scalar.activation(probs[:, ru % 2, kv], t_bank[kv % 2][:], ACT.Exp).then_inc(exp_done, 1)

            def copy_oT(u, ru, half):
                need(act, oT_ready, 2 * u + half + 1)
                need(act, o_ready, 2 * (u - 1) + half + 1)
                nc.scalar.activation(oT_sb[:, half], oT_bank[:], ACT.Copy).then_inc(oT_copied, 1)

            act.wait_ge(consts_loaded, 16 * CONST_DMAS)

            def phase(t, r):
                if live(t - 2):
                    exp(t - 2, (r - 2) % RING, 6)
                    exp(t - 2, (r - 2) % RING, 7)
                if live(t - 1):
                    exp(t - 1, (r - 1) % RING, 0)
                    exp(t - 1, (r - 1) % RING, 1)
                if live(t - 2):
                    copy_oT(t - 2, (r - 2) % RING, 1)
                if live(t - 1):
                    exp(t - 1, (r - 1) % RING, 2)
                    exp(t - 1, (r - 1) % RING, 3)
                u = t + 2
                if live(u):
                    layer = u // BATCH
                    need(act, qk_projected, u + 1)
                    need(act, split_step, SPLIT_STEPS * u)
                    need(act, parts_stored, 32 * (u - 1))
                    for k in range(KT):
                        for q in (qT[:, k * L:(k + 1) * L], q_parts[:, (r + 2) % 2, 0, k * L:(k + 1) * L]):
                            nc.scalar.activation(q, qk_bank[:, k * L:(k + 1) * L], ACT.Identity,
                                                 bias=bq_scaled[:, bass.ds(layer, 1), k], scale=SCALE).then_inc(qk_read, 1)
                    for kk in (kT[:], k_parts[:, (r + 2) % 2, 0]):
                        nc.scalar.activation(kk, qk_bank[0:KVD, D:D + S], ACT.Identity,
                                             bias=bk_sb[:, bass.ds(layer, 1)]).then_inc(qk_read, 1)
                if live(t - 1):
                    exp(t - 1, (r - 1) % RING, 4)
                u = t - 3
                if live(u):
                    need(act, yT_ready, u + 1)
                    nc.scalar.activation(xT_sb[:, :, u % BATCH], qk_bank[:, 0:KT * L].rearrange("p (k l) -> p k l", k=KT),
                                         ACT.Copy).then_inc(yT_copied, 1)
                if live(t - 1):
                    exp(t - 1, (r - 1) % RING, 5)
                    copy_oT(t - 1, (r - 1) % RING, 0)

            nc.scalar.activation(bq_scaled[:], bq_sb[:], ACT.Copy, scale=SCALE).then_inc(bias_scaled, 1)
            act.wait_ge(bias_scaled, 1)
            walk(act, phase)

        @block.vector
        def _(dve):
            nc.vector.memset(q_stack[64:P], 0.0).then_inc(pad_step, 1)
            nc.vector.memset(k_stack[64:MAX_ROW], 0.0).then_inc(pad_step, 1)
            nc.vector.memset(k_stack[MAX_ROW:P], 1.0).then_inc(pad_step, 1)
            nc.vector.memset(v_ones[:], 1.0).then_inc(pad_step, 1)
            dve.wait_ge(pad_step, 4)
            nc.vector.memset(recip[:], 0.0).then_inc(padded, 1)

            def flags():
                dve.wait_ge(all_masks_loaded, 16)
                nc.vector.tensor_reduce(mask_top[:], mask_sb[:], AX.XY, ALU.max,
                                        apply_absolute_value=True).then_inc(flag_step, 1)
                dve.wait_ge(flag_step, 2)
                nc.vector.tensor_scalar(mask_flag[:], mask_any[:], 0.0, None, ALU.not_equal).then_inc(flag_ready, 1)

            def maximum(u, ru, kv):
                need(dve, scores_ready, KV * u + kv + 1)
                need(dve, maxT_ready, u - 1)
                nc.vector.tensor_reduce(row_max[:, ru % 2, GROUP * kv:GROUP * (kv + 1)],
                                        s_bank[kv % 2][:].rearrange("p (g s) -> p g s", g=GROUP),
                                        AX.X, ALU.max).then_inc(max_done, 1)

            def max_rows(u, ru):
                m = misc_bank[0:HEADS, 0:L]
                parts = [max_parts[:, ru % 2, n] for n in range(PARTS)]
                need(dve, maxT_ready, u + 1)
                need(dve, max_rows_loaded, 16 * MAX_ROW_DMAS * (u - 1))
                nc.vector.tensor_scalar(parts[0], m, -1.0, None, ALU.mult).then_inc(maxT_step, 1)
                dve.wait_ge(maxT_step, MAXT_STEPS * u + 1)
                nc.vector.scalar_tensor_tensor(out=max_rest[:], in0=m, scalar=-1.0, in1=parts[0],
                                               op0=ALU.mult, op1=ALU.subtract).then_inc(maxT_step, 1)
                dve.wait_ge(maxT_step, MAXT_STEPS * u + 2)
                nc.vector.tensor_copy(parts[1], max_rest[:]).then_inc(maxT_step, 1)
                dve.wait_ge(maxT_step, MAXT_STEPS * u + 3)
                nc.vector.tensor_tensor(parts[2], max_rest[:], parts[1], ALU.subtract).then_inc(maxT_step, 1)

            def normalise(u, ru, half):
                o = o_bank[:].rearrange("p (n c) -> p n c", c=32)
                need(dve, o_ready, 2 * u + half + 1)
                nc.vector.reciprocal(recip[:, half], o[:, :, HD]).then_inc(recip_done, 1)
                dve.wait_ge(recip_done, 2 * u + half + 1)
                need(dve, attnT_ready, u)
                nc.vector.tensor_tensor(attn[:, half * P:(half + 1) * P].rearrange("p (n c) -> p n c", c=HD),
                                        o[:, :, 0:HD], recip[:, half].unsqueeze(2).broadcast_to([P, 16, HD]),
                                        ALU.mult).then_inc(o_normed, 1)

            def norm(u):
                done = NORM_STEPS * u
                need(dve, proj_ready, u + 1)
                need(dve, x_bo_ready, u + 1)
                nc.vector.tensor_tensor(z[:], misc_bank[:, 0:D], x_bo[:], ALU.add).then_inc(norm_step, 1)
                dve.wait_ge(norm_step, done + 1)
                nc.vector.bn_stats(stats[:], z[:]).then_inc(norm_step, 1)
                dve.wait_ge(norm_step, done + 2)
                nc.vector.memset(held_v[:], 0.0)
                nc.vector.bn_aggr(mean_var[:], stats[:]).then_inc(norm_step, 1)
                dve.wait_ge(norm_step, done + 3)
                nc.vector.tensor_scalar(var_eps[:], mean_var[:, 1:2], EPS, None, ALU.add).then_inc(norm_step, 1)

            def norm_end(u):
                need(dve, rstd_ready, u + 1)
                need(dve, affine_step, 2 * u - 1)
                nc.vector.tensor_scalar(normed[:], z[:], mean_var[:, 0:1], rstd[:, 0:1],
                                        ALU.subtract, ALU.mult).then_inc(norm_step, 1)

            def values(u, ru):
                need(dve, v_projected, u + 1)
                need(dve, oT_ready, 2 * (u - RING + 1))
                nc.vector.tensor_tensor(v_ones[:, ru, :, 0:HD], misc_bank[:, 0:KVD].rearrange("p (h d) -> p h d", d=HD),
                                        rows_sb[:, u // BATCH, 3 * D:3 * D + KVD].rearrange("p (h d) -> p h d", d=HD),
                                        ALU.add).then_inc(v_ready, 1)

            def phase(t, r):
                if live(t):
                    maximum(t, r, 0)
                    maximum(t, r, 1)
                    maximum(t, r, 2)
                if live(t - 2):
                    normalise(t - 2, (r - 2) % RING, 0)
                if live(t):
                    maximum(t, r, 3)
                    maximum(t, r, 4)
                if live(t - 3):
                    norm(t - 3)
                if live(t):
                    maximum(t, r, 5)
                    maximum(t, r, 6)
                if live(t - 3):
                    norm_end(t - 3)
                if live(t + 2):
                    values(t + 2, (r + 2) % RING)
                if live(t):
                    maximum(t, r, 7)
                if live(t - 2):
                    normalise(t - 2, (r - 2) % RING, 1)
                if live(t):
                    max_rows(t, r)
                if live(t - 2):
                    need(dve, attnT_ready, t - 1)
                    need(dve, proj_ready, t - 2)
                    nc.vector.tensor_copy(attnT[:], misc_bank[:, 0:D].rearrange("p (k l) -> p k l", k=KT)
                                          ).then_inc(attnT_copied, 1)

            flags()
            dve.wait_ge(consts_loaded, 16 * CONST_DMAS)
            dve.wait_ge(padded, 1)
            walk(dve, phase)

        @block.tensor
        def _(pe):
            def scores(u, ru, kv, masked):
                if kv == 0:
                    need(pe, stacks_loaded, 16 * STACK_DMAS * (u + 1))
                    if masked:
                        need(pe, mask_step, 4 * (u + 1))
                need(pe, max_done, KV * u + kv - 1)
                for g in range(GROUP):
                    mm = nc.tensor.matmul(s_bank[kv % 2][:, g * S:(g + 1) * S],
                                          q_stack[0:SCORE_ROWS, ru, GROUP * kv + g], k_stack[0:SCORE_ROWS, ru, kv],
                                          start=(g == 0), stop=(g == GROUP - 1 and not masked), skip_group_check=True)
                if masked:
                    for n in range(PARTS):
                        mm = nc.tensor.matmul(s_bank[kv % 2][:].rearrange("p (g s) -> p g s", g=GROUP), ident[:],
                                              mask_parts[:, ru, n:n + 1].broadcast_to([P, GROUP, S]),
                                              start=False, stop=(n == PARTS - 1), skip_group_check=True)
                mm.then_inc(scores_ready, 1)

            def scoresT(u, ru, kv, masked):
                if kv == 0:
                    need(pe, max_rows_loaded, 16 * MAX_ROW_DMAS * (u + 1))
                need(pe, exp_done, KV * u + kv - 1)
                mm = nc.tensor.matmul(t_bank[kv % 2][:], k_stack[0:STACK_ROWS, ru, kv],
                                      q_stack[0:STACK_ROWS, ru, GROUP * kv:GROUP * (kv + 1)],
                                      start=True, stop=not masked)
                if masked:
                    for n in range(PARTS):
                        mm = nc.tensor.matmul(t_bank[kv % 2][:].rearrange("p (g l) -> p g l", g=GROUP),
                                              mask_parts[:, ru, n], ident[:].unsqueeze(1).broadcast_to([P, GROUP, L]),
                                              start=False, stop=(n == PARTS - 1))
                mm.then_inc(scoresT_ready, 1)

            def project_v(u, ru):
                need(pe, w_loaded, 16 * (u // BATCH + 1))
                need(pe, ctx_loaded, 16 * (u + 1))
                if not isinstance(u, int) or u - 5 >= 0:
                    need(pe, norm_step, NORM_STEPS * (u - 5) + 1)
                else:
                    need(pe, v_ready, u)
                    if u >= 3:
                        need(pe, maxT_step, MAXT_STEPS * (u - 3) + 2)
                        need(pe, attnT_copied, u - 4)
                for k in range(KT):
                    mm = nc.tensor.matmul(misc_bank[:, 0:KVD], ctx_sb[:, ru, k], w_now[:, k, D + KVD:D + 2 * KVD],
                                          start=(k == 0), stop=(k == KT - 1))
                mm.then_inc(v_projected, 1)

            def project_qk(u, ru):
                need(pe, yT_copied, u - 5)
                if isinstance(u, int):
                    need(pe, qk_read, QK_READS * u)
                b = u % BATCH
                for n in range(KT):
                    for k in range(KT):
                        nc.tensor.matmul(qk_bank[:, n * L:(n + 1) * L], w_now[:, k, n * P:(n + 1) * P], xT_sb[:, k, b],
                                         start=(n == 0 and k == 0), stop=(k == KT - 1), skip_group_check=True)
                for k in range(KT):
                    mm = nc.tensor.matmul(qk_bank[0:KVD, D:D + S], w_now[:, k, D:D + KVD], ctx_sb[:, ru, k],
                                          start=False, stop=(k == KT - 1), skip_group_check=True)
                mm.then_inc(qk_projected, 1)

            def transpose_max(u, ru):
                need(pe, max_done, KV * (u + 1))
                need(pe, v_ready, upto(u + 2) + 1)
                if isinstance(u, int) and u >= 3:
                    need(pe, norm_step, NORM_STEPS * (u - 3) + 1)
                nc.tensor.transpose(misc_bank[0:HEADS, 0:L], row_max[:, ru % 2], identf[:]).then_inc(maxT_ready, 1)

            def probs_v(u, ru, half):
                need(pe, exp_done, KV * u + HALF * (half + 1))
                need(pe, oT_copied, 2 * u + half)
                for j in range(HALF):
                    kv = half * HALF + j
                    mm = nc.tensor.matmul(oT_bank[32 * j:32 * (j + 1)], v_ones[:, ru, kv], probs[:, ru % 2, kv],
                                          start=True, stop=True)
                mm.then_inc(oT_ready, 1)

            def transpose_o(u, half):
                need(pe, oT_copied, 2 * u + half + 1)
                need(pe, o_normed, 2 * u + half)
                for g in range(GROUP):
                    mm = nc.tensor.transpose(o_bank[:, g * P:(g + 1) * P], oT_sb[:, half, g * L:(g + 1) * L], identf[:])
                mm.then_inc(o_ready, 1)

            def transpose_attn(u):
                need(pe, o_normed, 2 * (u + 1))
                need(pe, maxT_step, MAXT_STEPS * upto(u + 2) + 2)
                if isinstance(u, int) and u >= 1:
                    need(pe, norm_step, NORM_STEPS * (u - 1) + 1)
                for k in range(KT):
                    mm = nc.tensor.transpose(misc_bank[:, k * L:(k + 1) * L], attn[:, k * P:(k + 1) * P], identf[:])
                mm.then_inc(attnT_ready, 1)

            def project_out(u):
                need(pe, attnT_copied, u + 1)
                for k in range(KT):
                    mm = nc.tensor.matmul(misc_bank[:, 0:D], attnT[:, k], wo_sb[:, u // BATCH, k],
                                          start=(k == 0), stop=(k == KT - 1))
                mm.then_inc(proj_ready, 1)

            def transpose_y(u, ru):
                need(pe, affine_step, 2 * (u + 1))
                need(pe, qk_read, QK_READS * (upto(u + 5) + 1))
                if isinstance(u, int):
                    need(pe, yT_copied, u)
                for k in range(KT):
                    mm = nc.tensor.transpose(qk_bank[:, k * L:(k + 1) * L], y[:, ru % 2, k * P:(k + 1) * P], identf[:])
                mm.then_inc(yT_ready, 1)

            pe.wait_ge(ident_step, 6)
            pe.wait_ge(xT_loaded, 16)

            def phase(t, r, masked):
                r1, r2, r3 = (r - 1) % RING, (r - 2) % RING, (r - 3) % RING
                if isinstance(t, int) and t == 0:
                    pe.wait_ge(padded, 1)
                now, before, last = live(t), live(t - 1), live(t - 2)
                if now:
                    scores(t, r, 0, None)
                    scores(t, r, 1, masked)
                if last:
                    scoresT(t - 2, r2, 6, None)
                if now:
                    scores(t, r, 2, masked)
                if last:
                    scoresT(t - 2, r2, 7, masked)
                    transpose_o(t - 2, 0)
                if now:
                    scores(t, r, 3, None)
                if before:
                    scoresT(t - 1, r1, 0, masked)
                if now:
                    scores(t, r, 4, masked)
                if live(t - 3):
                    project_out(t - 3)
                if now:
                    scores(t, r, 5, None)
                if before:
                    scoresT(t - 1, r1, 1, masked)
                if last:
                    probs_v(t - 2, r2, 1)
                if now:
                    scores(t, r, 6, None)
                if before:
                    scoresT(t - 1, r1, 2, masked)
                if live(t + 2):
                    project_v(t + 2, (r + 2) % RING)
                if now:
                    scores(t, r, 7, None)
                if before:
                    scoresT(t - 1, r1, 3, masked)
                if last:
                    transpose_o(t - 2, 1)
                if live(t + 2):
                    project_qk(t + 2, (r + 2) % RING)
                if before:
                    scoresT(t - 1, r1, 4, masked)
                if now:
                    transpose_max(t, r)
                if live(t - 3):
                    transpose_y(t - 3, r3)
                if before:
                    scoresT(t - 1, r1, 5, masked)
                    probs_v(t - 1, r1, 0)
                if last:
                    transpose_attn(t - 2)

            pe.wait_ge(flag_ready, 1)
            any_mask = pe.value_load(mask_flag[0:1, 0:1])
            with pe.If(any_mask):
                walk(pe, lambda t, r: phase(t, r, True))
            with pe.Else():
                walk(pe, lambda t, r: phase(t, r, False))


def kernel(**inputs):
    import concourse.bacc as bacc
    from concourse.bass_utils import run_bass_kernel_spmd

    def both(name):
        return [np.asarray(inputs[f"L{n}_xattn_{name}"]) for n in range(LAYERS)]

    q_order = np.arange(D).reshape(HEADS // 2, 2, HD).transpose(1, 2, 0).reshape(-1)
    k_order = np.arange(KVD).reshape(KV, HD).T.reshape(-1)
    o_order = np.arange(D).reshape(2, HALF, GROUP, HD).transpose(0, 2, 1, 3).reshape(-1)
    x, context = np.asarray(inputs["x"]), np.asarray(inputs["ctx_2048"])
    w_qkv = np.stack([np.concatenate([q[:, q_order], k[:, k_order], v], axis=1)
                      for q, k, v in zip(both("Wq"), both("Wk"), both("Wv"))])
    arrays = {
        "x": x,
        "xT": x.transpose(2, 0, 1),
        "ctxT": context.transpose(0, 2, 1),
        "mask": np.asarray(inputs["mask_Bx1xSxS2_ff0"]),
        "w_qkv": w_qkv,
        "w_o": np.stack([w[o_order] for w in both("Wo")]),
        "b_q": np.stack([b[q_order].reshape(KT, P) for b in both("bq")]).transpose(2, 0, 1),
        "b_k": np.stack([b[k_order] for b in both("bk")]).T,
        "rows": np.stack([np.concatenate(r) for r in zip(both("bo"), both("gamma"), both("beta"), both("bv"))]),
    }
    arrays["rows"] = arrays["rows"].reshape(-1)
    nc = bacc.Bacc("TRN2", target_bir_lowering=False, num_devices=1)
    arrays = {name: np.ascontiguousarray(a) for name, a in arrays.items()}
    args = [nc.dram_tensor(name, a.shape, mybir.dt.from_np(a.dtype), kind="ExternalInput").ap()
            for name, a in arrays.items()]
    result = nc.dram_tensor("result", (BATCH, L, D), F32, kind="ExternalOutput").ap()
    cross_attention(nc, *args, result)
    done = run_bass_kernel_spmd(nc, [arrays], core_ids=[0])
    return done.results[0]["result"]
```

```python
from contextlib import ExitStack

import concourse.bass as bass
import numpy as np
from concourse import mybir

F32 = mybir.dt.float32
BF16 = mybir.dt.bfloat16
I32 = mybir.dt.int32
ALU = mybir.AluOpType
ACT = mybir.ActivationFunctionType
AX = mybir.AxisListType

P = 128
LAYERS, BATCH, L, S, D = 2, 16, 128, 128, 256
HEADS, KV, HD = 32, 8, 8
GROUP = HEADS // KV
KT = D // P
UNITS = LAYERS * BATCH
PARTS = 3
TERM_ROWS = PARTS * PARTS * HD
SCORE_ROWS = 96
MAX_ROW = 96
STACK_ROWS = MAX_ROW + PARTS
RING = 4
HALF = KV // 2
KVD = KV * HD
SCALE = float(HD) ** -0.5
EPS = 1e-6
LOOPS = ((0, 4, 12), (1, 20, 28))
FIRST_PHASE, LAST_PHASE = -2, UNITS + 2


def live(u):
    return not isinstance(u, int) or 0 <= u < UNITS


def place(u, layer):
    return (u // BATCH, u % BATCH) if isinstance(u, int) else (layer, u - BATCH * layer)


def total(n, first, second, layer):
    if not isinstance(n, int):
        return n * first if layer == 0 else n * second + BATCH * (first - second)
    return first * min(n, BATCH) + second * max(n - BATCH, 0)


def need(engine, sem, count):
    if not isinstance(count, int) or count > 0:
        engine.wait_ge(sem, count)


def upto(u):
    return min(u, UNITS - 1) if isinstance(u, int) else u


def walk(engine, phase, first=FIRST_PHASE):
    for layer, start, end in LOOPS:
        for t in range(first, start + 1):
            phase(0, t, None)
        with engine.Fori(start, end - RING + 1, RING) as turn:
            for step in range(1, RING + 1):
                phase(turn, step, layer)
        first = end + 1
    for t in range(first, LAST_PHASE + 1):
        phase(0, t, None)


def cross_attention(nc, x, xT, ctxT, mask, w_q, w_kv, w_o, b_q, b_k, rows, out):
    with ExitStack() as ctx:
        def sb(name, shape, dt):
            return ctx.enter_context(nc.sbuf_tensor(name, shape, dt))

        def sem(name):
            return ctx.enter_context(nc.semaphore(name))

        q_scratch = nc.dram_tensor("q_scratch", (UNITS, PARTS, P, KT * L), BF16).ap()
        k_scratch = nc.dram_tensor("k_scratch", (BATCH, PARTS, LAYERS * KVD, S), BF16).ap()

        x_sb = sb("x_sb", [P, BATCH, D], F32)
        xT_sb = sb("xT_sb", [P, KT, BATCH, L], F32)
        ctx_sb = sb("ctx_sb", [P, RING, KT, S], F32)
        mask_sb = sb("mask_sb", [P, BATCH, S], F32)
        mask_parts = sb("mask_parts", [P, RING, PARTS, S], BF16)
        wq_sb = sb("wq_sb", [P, LAYERS, KT, D], F32)
        wkv_sb = sb("wkv_sb", [P, KT, 2, LAYERS * KVD], F32)
        wo_sb = sb("wo_sb", [P, LAYERS, KT, D], F32)
        bq_sb = sb("bq_sb", [P, LAYERS, KT], F32)
        bq_scaled = sb("bq_scaled", [P, LAYERS, KT], F32)
        bk_sb = sb("bk_sb", [LAYERS * KVD, 1], F32)
        rows_sb = sb("rows_sb", [P, LAYERS, 3 * D + KVD], F32)
        identf = sb("identf", [P, P], F32)
        ident = sb("ident", [P, P], BF16)
        qT = sb("qT", [P, KT * L], F32)
        kT = sb("kT", [P, S], F32)
        q_rest = sb("q_rest", [P, KT * L], F32)
        k_rest = sb("k_rest", [P, S], F32)
        mask_now = sb("mask_now", [P, 2, S], F32)
        zeros = sb("zeros", [P, S], F32)
        held = sb("held", [P, RING], F32)
        held_v = sb("held_v", [P, 1], F32)
        m_rest = sb("m_rest", [P, S], F32)
        q_parts = sb("q_parts", [P, 2, PARTS, KT * L], BF16)
        k_parts = sb("k_parts", [P, 2, PARTS, S], BF16)
        q_stack = sb("q_stack", [P, RING, HEADS, L], BF16)
        k_stack = sb("k_stack", [P, RING, KV, S], BF16)
        row_max = sb("row_max", [P, 2, PARTS * HEADS], F32)
        max_rest = sb("max_rest", [PARTS * HEADS, L], F32)
        max_parts = sb("max_parts", [PARTS * HEADS, 2, L], BF16)
        v_ones = sb("v_ones", [P, RING, KV, 32], F32)
        v_next = sb("v_next", [P, BATCH, KVD], F32)
        probs = sb("probs", [P, 2, KV, GROUP * L], F32)
        oT_sb = sb("oT_sb", [P, 2, GROUP * L], F32)
        recip = sb("recip", [P, 2, 16], F32)
        attn = sb("attn", [P, D], F32)
        attnT = sb("attnT", [P, KT, L], F32)
        x_bo = sb("x_bo", [P, D], F32)
        z = sb("z", [P, D], F32)
        stats = sb("stats", [P, 6], F32)
        mean_var = sb("mean_var", [P, 2], F32)
        var_eps = sb("var_eps", [P, 1], F32)
        minus_half = sb("minus_half", [P, 1], F32)
        rstd = sb("rstd", [P, 1], F32)
        normed = sb("normed", [P, D], F32)
        scaled = sb("scaled", [P, D], F32)
        y = sb("y", [P, 2, D], F32)
        mask_top = sb("mask_top", [P, 1], F32)
        mask_any = sb("mask_any", [P, 1], F32)
        mask_flag = sb("mask_flag", [P, 1], I32)

        def bank(name):
            return ctx.enter_context(nc.psum_tensor(name, [P, 512], F32))

        s_bank = [bank("s_bank0"), bank("s_bank1")]
        t_bank = [bank("t_bank0"), bank("t_bank1")]
        oT_bank = bank("oT_bank")
        o_bank = bank("o_bank")
        qk_bank = bank("qk_bank")
        misc_bank = bank("misc_bank")

        weights_loaded = sem("weights_loaded")
        consts_loaded = sem("consts_loaded")
        xT_loaded = sem("xT_loaded")
        x_loaded = sem("x_loaded")
        mask_loaded = sem("mask_loaded")
        all_masks_loaded = sem("all_masks_loaded")
        ctx_loaded = sem("ctx_loaded")
        ident_step = sem("ident_step")
        pad_step = sem("pad_step")
        padded = sem("padded")
        bias_scaled = sem("bias_scaled")
        flag_step = sem("flag_step")
        flag_ready = sem("flag_ready")
        mask_step = sem("mask_step")
        qk_projected = sem("qk_projected")
        v_projected = sem("v_projected")
        qk_read = sem("qk_read")
        v_ready = sem("v_ready")
        v_next_ready = sem("v_next_ready")
        split_step = sem("split_step")
        parts_stored = sem("parts_stored")
        stacks_loaded = sem("stacks_loaded")
        scores_ready = sem("scores_ready")
        max_done = sem("max_done")
        max_copied = sem("max_copied")
        maxT_ready = sem("maxT_ready")
        maxT_step = sem("maxT_step")
        max_rows_loaded = sem("max_rows_loaded")
        scoresT_ready = sem("scoresT_ready")
        exp_done = sem("exp_done")
        oT_ready = sem("oT_ready")
        oT_copied = sem("oT_copied")
        o_ready = sem("o_ready")
        recip_done = sem("recip_done")
        o_normed = sem("o_normed")
        attnT_ready = sem("attnT_ready")
        attnT_copied = sem("attnT_copied")
        proj_ready = sem("proj_ready")
        x_bo_ready = sem("x_bo_ready")
        rstd_ready = sem("rstd_ready")
        norm_step = sem("norm_step")
        affine_step = sem("affine_step")
        yT_ready = sem("yT_ready")
        yT_copied = sem("yT_copied")
        y_left = sem("y_left")

        MAXT_STEPS, NORM_STEPS = 4, 5
        SPLITS, QK_READS, STORES = (6, 3), (6, 4), (32, 16)
        STACK_DMAS = 6
        CONST_DMAS = 3
        block = ctx.enter_context(nc.Block())

        @block.sync
        def _(sp):
            FIRST_X = 2
            xT_d = xT.rearrange("(k p) b l -> p k b l", p=P)
            sp.dma_start(wq_sb[:, 0], w_q[0].rearrange("(k p) n -> p k n", p=P)).then_inc(weights_loaded, 16)
            sp.dma_start(xT_sb[:, :, 0:FIRST_X], xT_d[:, :, 0:FIRST_X]).then_inc(weights_loaded, 16)
            sp.dma_start(ctx_sb[:, 0], ctxT[0].rearrange("(k p) s -> p k s", p=P)).then_inc(ctx_loaded, 16)
            sp.dma_start(wkv_sb[:].rearrange("p k a n -> p k (a n)"),
                         w_kv.rearrange("(k p) n -> p k n", p=P)).then_inc(weights_loaded, 16)
            sp.dma_start(bq_sb[:], b_q).then_inc(consts_loaded, 16)
            sp.dma_start(bk_sb[:], b_k).then_inc(consts_loaded, 16)
            sp.dma_start(rows_sb[:].rearrange("p a n -> p (a n)"), rows.partition_broadcast(P)).then_inc(consts_loaded, 16)
            sp.dma_start(mask_sb[:], mask.rearrange("b o l s -> l (b o) s")).then_inc(all_masks_loaded, 16)

            def phase(turn, step, loop_layer):
                t, r = turn + step, step % RING

                def of(per, k):
                    return turn * per + per * (step + k)

                def of_layers(per, k):
                    if isinstance(turn, int):
                        return total(t + k, *per, None)
                    return turn * per[loop_layer] + (per[loop_layer] * (step + k) + loop_layer * BATCH * (per[0] - per[1]))

                if not isinstance(turn, int):
                    for count in (of(1, 0), of(16, 3), of(4, 1), of(2, -2), of(16, -3), of(1, -2), of(16 * STACK_DMAS, 2),
                                  of_layers(SPLITS, 3), of(MAXT_STEPS, 1), of(16, 0), of(KV, 1 - RING),
                                  of_layers(STORES, 3), of(KV, 3 - RING)):
                        sp.to_reg(count)
                if live(t):
                    need(sp, maxT_step, of(MAXT_STEPS, 1))
                    need(sp, max_rows_loaded, of(16, 0))
                    need(sp, scoresT_ready, of(KV, 1 - RING))
                    sp.dma_start(q_stack[MAX_ROW:MAX_ROW + PARTS, r], max_parts[:, r % 2].rearrange("p (o l) -> p o l", o=1)
                                 ).then_inc(max_rows_loaded, 16)
                u, ru = t + 2, (r + 2) % RING
                layer, b = place(u, loop_layer)
                if live(u):
                    need(sp, stacks_loaded, of(16 * STACK_DMAS, 2))
                    need(sp, split_step, of_layers(SPLITS, 3))
                    sp.dma_start(q_scratch[u].rearrange("a p n -> p a n"), q_parts[:, ru % 2]).then_inc(parts_stored, 16)
                    if layer == 0:
                        sp.dma_start(k_scratch[b].rearrange("a p n -> p a n"), k_parts[:, ru % 2]
                                     ).then_inc(parts_stored, 16)
                layer, b = place(t + 3, loop_layer)
                if live(t + 3) and layer == 0:
                    need(sp, qk_projected, of(1, 0))
                    need(sp, v_projected, of(1, 0))
                    need(sp, ctx_loaded, of(16, 3))
                    sp.dma_start(ctx_sb[:, (r + 3) % RING], ctxT[b].rearrange("(k p) s -> p k s", p=P)
                                 ).then_inc(ctx_loaded, 16)
                u, ru = t + 2, (r + 2) % RING
                if live(u):
                    need(sp, mask_step, of(4, 1))
                    sp.dma_start(mask_now[:, ru % 2], mask[place(u, loop_layer)[1], 0]).then_inc(mask_loaded, 16)
                u, ru = t - 3, (r - 3) % RING
                if live(u):
                    layer, b = place(u, loop_layer)
                    need(sp, affine_step, of(2, -2))
                    need(sp, y_left, of(16, -3))
                    if layer == LAYERS - 1:
                        sp.dma_start(out[b], y[:, ru % 2]).then_inc(y_left, 16)
                    else:
                        need(sp, x_bo_ready, of(1, -2))
                        sp.dma_start(x_sb[:, b], y[:, ru % 2]).then_inc(y_left, 16)
                if isinstance(t, int) and t == FIRST_PHASE:
                    sp.dma_start(xT_sb[:, :, FIRST_X:], xT_d[:, :, FIRST_X:]).then_inc(xT_loaded, 16)
                    sp.dma_start(x_sb[:], x.rearrange("b l d -> l b d")).then_inc(x_loaded, 16)
                    sp.dma_start(wo_sb[:], w_o.rearrange("a (k p) n -> p a k n", p=P)).then_inc(xT_loaded, 16)
                    sp.dma_start(wq_sb[:, 1], w_q[1].rearrange("(k p) n -> p k n", p=P)).then_inc(xT_loaded, 16)
                u, ru = t + 2, (r + 2) % RING
                layer, b = place(u, loop_layer)
                if live(u):
                    need(sp, parts_stored, of_layers(STORES, 3))
                    need(sp, scoresT_ready, of(KV, 3 - RING))
                    if isinstance(u, int) and u < RING:
                        need(sp, padded, 1)
                    q_rows = q_scratch[u].rearrange("a (d h) n -> (a d) (h n)", d=HD)
                    for part in range(PARTS):
                        first = part * PARTS * HD
                        sp.dma_start(q_stack[first:first + PARTS * HD, ru].rearrange("p h l -> p (h l)"),
                                     q_rows).then_inc(stacks_loaded, 16)
                        k_rows = k_scratch[b, part, layer * KVD:(layer + 1) * KVD].rearrange("(d h) n -> d (h n)", d=HD)
                        sp.dma_start(k_stack[first:first + PARTS * HD, ru].rearrange("p h l -> p (h l)"),
                                     k_rows.partition_broadcast(PARTS)).then_inc(stacks_loaded, 16)

            walk(sp, phase)
            sp.wait_ge(y_left, 16 * UNITS)
            sp.wait_ge(parts_stored, total(UNITS, *STORES, None))

        @block.gpsimd
        def _(pool):
            nc.gpsimd.memset(identf[:], 0.0).then_inc(ident_step, 1)
            nc.gpsimd.memset(ident[:], 0.0).then_inc(ident_step, 1)
            pool.wait_ge(ident_step, 2)
            nc.gpsimd.memset(zeros[:], 0.0).then_inc(ident_step, 1)
            nc.gpsimd.memset(minus_half[:], -0.5).then_inc(ident_step, 1)
            for m in (identf, ident):
                nc.gpsimd.affine_select(out=m[:], in_=m[:], compare_op=ALU.not_equal, fill=1.0, base=0,
                                        pattern=[[-1, P]], channel_multiplier=1).then_inc(ident_step, 1)

            def flags():
                pool.wait_ge(flag_step, 1)
                nc.gpsimd.partition_all_reduce(mask_any[:], mask_top[:], P, bass.bass_isa.ReduceOp.max).then_inc(flag_step, 1)

            def split(f, rest, parts, step, done):
                nc.gpsimd.tensor_tensor(rest, f, parts[0], ALU.subtract).then_inc(step, 1)
                nc.gpsimd.tensor_tensor(parts[1], f, parts[0], ALU.subtract).then_inc(step, 1)
                pool.wait_ge(step, done + 2)
                nc.gpsimd.tensor_tensor(parts[2], rest, parts[1], ALU.subtract).then_inc(step, 1)

            def hold(n):
                nc.gpsimd.tensor_tensor(held[:, n:n + 1], minus_half[:], minus_half[:], ALU.add)

            def phase(turn, step, loop_layer):
                t, r = turn + step, step % RING
                u, ru = t + 1, (r + 1) % RING
                if live(u):
                    need(pool, mask_loaded, 16 * (u + 1))
                    need(pool, scoresT_ready, KV * (u - RING + 1))
                    parts = [mask_parts[:, ru, n] for n in range(PARTS)]
                    nc.gpsimd.tensor_tensor(parts[0], mask_now[:, ru % 2], zeros[:], ALU.add).then_inc(mask_step, 1)
                    pool.wait_ge(mask_step, 4 * u + 1)
                    split(mask_now[:, ru % 2], m_rest[:], parts, mask_step, 4 * u + 1)
                u = t - 3
                if live(u):
                    layer, b = place(u, loop_layer)
                    need(pool, norm_step, NORM_STEPS * u + 4)
                    nc.gpsimd.tensor_tensor(rstd[:], var_eps[:], minus_half[:], ALU.pow).then_inc(rstd_ready, 1)
                    need(pool, norm_step, NORM_STEPS * (u + 1))
                    need(pool, affine_step, 2 * u)
                    nc.gpsimd.tensor_tensor(scaled[:], normed[:], rows_sb[:, layer, D:2 * D],
                                            ALU.mult).then_inc(affine_step, 1)
                    if not isinstance(u, int) and layer == 0 or isinstance(u, int) and u - 2 < BATCH:
                        need(pool, yT_ready, u - 1)
                    need(pool, y_left, 16 * (u - 1))
                    pool.wait_ge(affine_step, 2 * u + 1)
                    nc.gpsimd.tensor_tensor(y[:, (r - 3) % 2], scaled[:], rows_sb[:, layer, 2 * D:3 * D],
                                            ALU.add).then_inc(affine_step, 1)
                u, ru = t + 2, (r + 2) % RING
                if live(u):
                    layer, b = place(u, loop_layer)
                    need(pool, qk_read, total(u + 1, *QK_READS, loop_layer))
                    done = total(u, *SPLITS, loop_layer)
                    split(qT[:], q_rest[:], [q_parts[:, ru % 2, n] for n in range(PARTS)], split_step, done)
                    if layer == 0:
                        split(kT[:], k_rest[:], [k_parts[:, ru % 2, n] for n in range(PARTS)], split_step, done + 3)
                u = t - 2
                if live(u):
                    layer, b = place(u, loop_layer)
                    if isinstance(u, int) and u == 0:
                        pool.wait_ge(x_loaded, 16)
                        pool.wait_ge(consts_loaded, 16 * CONST_DMAS)
                    need(pool, norm_step, NORM_STEPS * (u - 1) + 1)
                    hold(step % RING)
                    nc.gpsimd.tensor_tensor(x_bo[:], x_sb[:, b], rows_sb[:, layer, 0:D], ALU.add).then_inc(x_bo_ready, 1)

            pool.wait_ge(ident_step, 6)
            flags()
            walk(pool, phase)

        @block.scalar
        def _(act):
            def exp(u, ru, kv):
                need(act, scoresT_ready, KV * u + kv + 1)
                need(act, oT_ready, 2 * (u - 2) + kv // HALF + 1)
                nc.scalar.activation(probs[:, ru % 2, kv], t_bank[kv % 2][:], ACT.Exp).then_inc(exp_done, 1)

            def copy_oT(u, ru, half):
                need(act, oT_ready, 2 * u + half + 1)
                need(act, o_ready, 2 * (u - 1) + half + 1)
                nc.scalar.activation(oT_sb[:, half], oT_bank[:], ACT.Copy).then_inc(oT_copied, 1)

            def phase(turn, step, loop_layer):
                t, r = turn + step, step % RING
                r1, r2 = (r - 1) % RING, (r - 2) % RING
                before, last = live(t - 1), live(t - 2)
                if last:
                    exp(t - 2, r2, 5)
                u = t - 4
                layer, b = place(u, loop_layer)
                if live(u) and layer == 0:
                    need(act, yT_ready, u + 1)
                    nc.scalar.activation(xT_sb[:, :, b], qk_bank[:, 0:KT * L].rearrange("p (k l) -> p k l", k=KT),
                                         ACT.Copy).then_inc(yT_copied, 1)
                if last:
                    copy_oT(t - 2, r2, 0)
                    exp(t - 2, r2, 6)
                if live(t - 3):
                    need(act, attnT_ready, t - 2)
                    need(act, proj_ready, t - 3)
                    nc.scalar.activation(attnT[:], o_bank[:, 0:D].rearrange("p (k l) -> p k l", k=KT),
                                         ACT.Copy).then_inc(attnT_copied, 1)
                if last:
                    exp(t - 2, r2, 7)
                if before:
                    exp(t - 1, r1, 0)
                    exp(t - 1, r1, 1)
                u, ru = t + 2, (r + 2) % RING
                layer, b = place(u, loop_layer)
                if live(u):
                    need(act, qk_projected, u + 1)
                    need(act, split_step, total(u, *SPLITS, loop_layer))
                    need(act, parts_stored, total(u - 1, *STORES, loop_layer))
                    for k in range(KT):
                        for q in (qT[:, k * L:(k + 1) * L], q_parts[:, ru % 2, 0, k * L:(k + 1) * L]):
                            nc.scalar.activation(q, qk_bank[:, k * L:(k + 1) * L], ACT.Identity,
                                                 bias=bq_scaled[:, layer, k:k + 1], scale=SCALE).then_inc(qk_read, 1)
                if before:
                    exp(t - 1, r1, 2)
                if live(u) and layer == 0:
                    for kk in (kT[:], k_parts[:, ru % 2, 0]):
                        nc.scalar.activation(kk, qk_bank[:, D:D + S], ACT.Identity, bias=bk_sb[:, 0:1]).then_inc(qk_read, 1)
                if before:
                    exp(t - 1, r1, 3)
                if last:
                    copy_oT(t - 2, r2, 1)
                if before:
                    exp(t - 1, r1, 4)

            act.wait_ge(consts_loaded, 16 * CONST_DMAS)
            nc.scalar.activation(bq_scaled[:], bq_sb[:], ACT.Copy, scale=SCALE).then_inc(bias_scaled, 1)
            act.wait_ge(bias_scaled, 1)
            walk(act, phase)

        @block.vector
        def _(dve):
            nc.vector.memset(q_stack[64:P], 0.0).then_inc(pad_step, 1)
            nc.vector.memset(k_stack[64:MAX_ROW], 0.0).then_inc(pad_step, 1)
            nc.vector.memset(k_stack[MAX_ROW:P], 1.0).then_inc(pad_step, 1)
            nc.vector.memset(v_ones[:], 1.0).then_inc(pad_step, 1)
            dve.wait_ge(pad_step, 4)
            nc.vector.memset(recip[:], 0.0).then_inc(padded, 1)

            def flags():
                dve.wait_ge(all_masks_loaded, 16)
                nc.vector.tensor_reduce(mask_top[:], mask_sb[:], AX.XY, ALU.max,
                                        apply_absolute_value=True).then_inc(flag_step, 1)
                dve.wait_ge(flag_step, 2)
                nc.vector.tensor_scalar(mask_flag[:], mask_any[:], 0.0, None, ALU.not_equal).then_inc(flag_ready, 1)

            def maximum(u, ru, kv):
                need(dve, scores_ready, KV * u + kv + 1)
                need(dve, maxT_ready, u - 1)
                nc.vector.tensor_reduce(row_max[:, ru % 2, GROUP * kv:GROUP * (kv + 1)],
                                        s_bank[kv % 2][:].rearrange("p (g s) -> p g s", g=GROUP),
                                        AX.X, ALU.max).then_inc(max_done, 1)

            def copy_max(u, ru):
                dve.wait_ge(max_done, KV * (u + 1))
                nc.vector.tensor_copy(row_max[:, ru % 2, HEADS:].rearrange("p (c h) -> p c h", h=HEADS),
                                      row_max[:, ru % 2, 0:HEADS].unsqueeze(1).broadcast_to([P, PARTS - 1, HEADS])
                                      ).then_inc(max_copied, 1)

            def max_rows(u, ru):
                m, parts = misc_bank[0:PARTS * HEADS, 0:L], max_parts[:, ru % 2]
                need(dve, maxT_ready, u + 1)
                need(dve, max_rows_loaded, 16 * (u - 1))
                nc.vector.tensor_scalar(parts, m, -1.0, None, ALU.mult).then_inc(maxT_step, 1)
                dve.wait_ge(maxT_step, MAXT_STEPS * u + 1)
                nc.vector.scalar_tensor_tensor(out=max_rest[:], in0=m, scalar=-1.0, in1=parts,
                                               op0=ALU.mult, op1=ALU.subtract).then_inc(maxT_step, 1)
                dve.wait_ge(maxT_step, MAXT_STEPS * u + 2)
                nc.vector.tensor_copy(parts[0:2 * HEADS], max_rest[0:2 * HEADS]).then_inc(maxT_step, 1)
                dve.wait_ge(maxT_step, MAXT_STEPS * u + 3)
                nc.vector.tensor_tensor(parts[0:HEADS], max_rest[0:HEADS], parts[0:HEADS], ALU.subtract
                                        ).then_inc(maxT_step, 1)

            def normalise(u, ru, half):
                o = o_bank[:].rearrange("p (n c) -> p n c", c=32)
                need(dve, o_ready, 2 * u + half + 1)
                nc.vector.reciprocal(recip[:, half], o[:, :, HD]).then_inc(recip_done, 1)
                dve.wait_ge(recip_done, 2 * u + half + 1)
                need(dve, attnT_ready, u)
                nc.vector.tensor_tensor(attn[:, half * P:(half + 1) * P].rearrange("p (n c) -> p n c", c=HD),
                                        o[:, :, 0:HD], recip[:, half].unsqueeze(2).broadcast_to([P, 16, HD]),
                                        ALU.mult).then_inc(o_normed, 1)

            def norm(u):
                done = NORM_STEPS * u
                need(dve, proj_ready, u + 1)
                need(dve, x_bo_ready, u + 1)
                nc.vector.tensor_tensor(z[:], misc_bank[:, 0:D], x_bo[:], ALU.add).then_inc(norm_step, 1)
                dve.wait_ge(norm_step, done + 1)
                nc.vector.bn_stats(stats[:], z[:]).then_inc(norm_step, 1)
                dve.wait_ge(norm_step, done + 2)
                nc.vector.memset(held_v[:], 0.0)
                nc.vector.bn_aggr(mean_var[:], stats[:]).then_inc(norm_step, 1)
                dve.wait_ge(norm_step, done + 3)
                nc.vector.tensor_scalar(var_eps[:], mean_var[:, 1:2], EPS, None, ALU.add).then_inc(norm_step, 1)

            def norm_end(u):
                need(dve, rstd_ready, u + 1)
                need(dve, affine_step, 2 * u - 1)
                nc.vector.tensor_scalar(normed[:], z[:], mean_var[:, 0:1], rstd[:, 0:1],
                                        ALU.subtract, ALU.mult).then_inc(norm_step, 1)

            def values(u, ru, layer, b):
                def heads(v):
                    return v.rearrange("p (h d) -> p h d", d=HD)

                need(dve, oT_ready, 2 * (u - RING + 1))
                if layer == 0:
                    need(dve, v_projected, u + 1)
                    bias = rows_sb[:, :, 3 * D:3 * D + KVD]
                    nc.vector.tensor_tensor(v_next[:, b], misc_bank[:, KVD:2 * KVD], bias[:, 1], ALU.add
                                            ).then_inc(v_next_ready, 1)
                    nc.vector.tensor_tensor(v_ones[:, ru, :, 0:HD], heads(misc_bank[:, 0:KVD]), heads(bias[:, 0]), ALU.add
                                            ).then_inc(v_ready, 1)
                else:
                    if isinstance(u, int) and u == BATCH:
                        need(dve, v_next_ready, BATCH)
                    nc.vector.tensor_copy(v_ones[:, ru, :, 0:HD], heads(v_next[:, b])).then_inc(v_ready, 1)

            def phase(turn, step, loop_layer):
                t, r = turn + step, step % RING
                if live(t):
                    maximum(t, r, 0)
                    maximum(t, r, 1)
                    maximum(t, r, 2)
                if live(t - 2):
                    normalise(t - 2, (r - 2) % RING, 0)
                if live(t):
                    maximum(t, r, 3)
                if live(t - 3):
                    norm(t - 3)
                if live(t):
                    maximum(t, r, 4)
                    maximum(t, r, 5)
                if live(t - 3):
                    norm_end(t - 3)
                if live(t):
                    maximum(t, r, 6)
                if live(t + 2):
                    values(t + 2, (r + 2) % RING, *place(t + 2, loop_layer))
                if live(t):
                    maximum(t, r, 7)
                    copy_max(t, r)
                if live(t - 2):
                    normalise(t - 2, (r - 2) % RING, 1)
                if live(t):
                    max_rows(t, r)

            flags()
            dve.wait_ge(consts_loaded, 16 * CONST_DMAS)
            dve.wait_ge(padded, 1)
            walk(dve, phase)

        @block.tensor
        def _(pe):
            def scores(u, ru, kv, masked):
                if kv == 0:
                    need(pe, stacks_loaded, 16 * STACK_DMAS * (u + 1))
                    if masked:
                        need(pe, mask_step, 4 * (u + 1))
                need(pe, max_done, KV * u + kv - 1)
                for g in range(GROUP):
                    mm = nc.tensor.matmul(s_bank[kv % 2][:, g * S:(g + 1) * S],
                                          q_stack[0:SCORE_ROWS, ru, GROUP * kv + g], k_stack[0:SCORE_ROWS, ru, kv],
                                          start=(g == 0), stop=(g == GROUP - 1 and not masked), skip_group_check=True)
                if masked:
                    for n in range(PARTS):
                        mm = nc.tensor.matmul(s_bank[kv % 2][:].rearrange("p (g s) -> p g s", g=GROUP), ident[:],
                                              mask_parts[:, ru, n:n + 1].broadcast_to([P, GROUP, S]),
                                              start=False, stop=(n == PARTS - 1), skip_group_check=True)
                mm.then_inc(scores_ready, 1)

            def scoresT(u, ru, kv, masked):
                if kv == 0:
                    need(pe, max_rows_loaded, 16 * (u + 1))
                need(pe, exp_done, KV * u + kv - 1)
                mm = nc.tensor.matmul(t_bank[kv % 2][:], k_stack[0:STACK_ROWS, ru, kv],
                                      q_stack[0:STACK_ROWS, ru, GROUP * kv:GROUP * (kv + 1)],
                                      start=True, stop=not masked)
                if masked:
                    for n in range(PARTS):
                        mm = nc.tensor.matmul(t_bank[kv % 2][:].rearrange("p (g l) -> p g l", g=GROUP),
                                              mask_parts[:, ru, n], ident[:].unsqueeze(1).broadcast_to([P, GROUP, L]),
                                              start=False, stop=(n == PARTS - 1))
                mm.then_inc(scoresT_ready, 1)

            def project_v(u, ru):
                need(pe, ctx_loaded, 16 * (u + 1))
                if not isinstance(u, int) or u >= 5:
                    need(pe, norm_step, NORM_STEPS * (u - 5) + 1)
                elif u >= 3:
                    need(pe, maxT_step, MAXT_STEPS * (u - 3) + 2)
                else:
                    need(pe, v_ready, u)
                for k in range(KT):
                    mm = nc.tensor.matmul(misc_bank[:, 0:LAYERS * KVD], ctx_sb[:, ru, k], wkv_sb[:, k, 1],
                                          start=(k == 0), stop=(k == KT - 1))
                mm.then_inc(v_projected, 1)

            def project_qk(u, ru, layer, b):
                if isinstance(u, int):
                    need(pe, yT_copied, min(u - 5, BATCH))
                    need(pe, qk_read, total(u, *QK_READS, None))
                elif layer == 0:
                    need(pe, yT_copied, u - 5)
                else:
                    need(pe, qk_read, total(u, *QK_READS, layer))
                if isinstance(u, int) and u == 0:
                    pe.wait_ge(weights_loaded, 48)
                    pe.wait_ge(ctx_loaded, 16)
                if isinstance(u, int) and u == 2:
                    pe.wait_ge(xT_loaded, 48)
                for n in range(KT):
                    for k in range(KT):
                        mm = nc.tensor.matmul(qk_bank[:, n * L:(n + 1) * L], wq_sb[:, layer, k, n * P:(n + 1) * P],
                                              xT_sb[:, k, b],
                                              start=(n == 0 and k == 0), stop=(k == KT - 1), skip_group_check=True)
                if layer == 0:
                    need(pe, ctx_loaded, 16 * (u + 1))
                    for k in range(KT):
                        mm = nc.tensor.matmul(qk_bank[:, D:D + S], wkv_sb[:, k, 0], ctx_sb[:, ru, k],
                                              start=False, stop=(k == KT - 1), skip_group_check=True)
                mm.then_inc(qk_projected, 1)

            def transpose_max(u, ru, layer):
                need(pe, max_copied, u + 1)
                if not isinstance(u, int) and layer == 0 or isinstance(u, int) and u + 2 < BATCH:
                    need(pe, v_ready, u + 3)
                else:
                    need(pe, norm_step, NORM_STEPS * (u - 3) + 1)
                nc.tensor.transpose(misc_bank[0:PARTS * HEADS, 0:L], row_max[:, ru % 2],
                                    identf[:]).then_inc(maxT_ready, 1)

            def probs_v(u, ru, half):
                need(pe, exp_done, KV * u + HALF * (half + 1))
                need(pe, oT_copied, 2 * u + half)
                for j in range(HALF):
                    kv = half * HALF + j
                    mm = nc.tensor.matmul(oT_bank[32 * j:32 * (j + 1)], v_ones[:, ru, kv], probs[:, ru % 2, kv],
                                          start=True, stop=True)
                mm.then_inc(oT_ready, 1)

            def transpose_o(u, half):
                need(pe, oT_copied, 2 * u + half + 1)
                if half == 1:
                    need(pe, o_normed, 2 * u + 1)
                else:
                    need(pe, attnT_copied, u)
                for g in range(GROUP):
                    mm = nc.tensor.transpose(o_bank[:, g * P:(g + 1) * P], oT_sb[:, half, g * L:(g + 1) * L], identf[:])
                mm.then_inc(o_ready, 1)

            def transpose_attn(u):
                need(pe, o_normed, 2 * (u + 1))
                for k in range(KT):
                    mm = nc.tensor.transpose(o_bank[:, k * L:(k + 1) * L], attn[:, k * P:(k + 1) * P], identf[:])
                mm.then_inc(attnT_ready, 1)

            def project_out(u, layer):
                need(pe, attnT_copied, u + 1)
                need(pe, maxT_step, MAXT_STEPS * upto(u + 2) + 2)
                if isinstance(u, int):
                    need(pe, norm_step, NORM_STEPS * (u - 1) + 1)
                for k in range(KT):
                    mm = nc.tensor.matmul(misc_bank[:, 0:D], attnT[:, k], wo_sb[:, layer, k],
                                          start=(k == 0), stop=(k == KT - 1))
                mm.then_inc(proj_ready, 1)

            def transpose_y(u, ru, layer):
                need(pe, affine_step, 2 * (u + 1))
                need(pe, qk_read, total(u + 6, *QK_READS, layer))
                for k in range(KT):
                    mm = nc.tensor.transpose(qk_bank[:, k * L:(k + 1) * L], y[:, ru % 2, k * P:(k + 1) * P], identf[:])
                mm.then_inc(yT_ready, 1)

            def phase(turn, step, loop_layer, masked):
                t, r = turn + step, step % RING
                r1, r2, r3 = (r - 1) % RING, (r - 2) % RING, (r - 3) % RING
                if isinstance(t, int) and t == 0:
                    pe.wait_ge(padded, 1)
                now, before, last = live(t), live(t - 1), live(t - 2)
                ahead, ra, (layer_ahead, b_ahead) = live(t + 2), (r + 2) % RING, place(t + 2, loop_layer)
                if now:
                    scores(t, r, 0, masked)
                if last:
                    scoresT(t - 2, r2, 5, masked)
                    probs_v(t - 2, r2, 0)
                layer_y = place(t - 4, loop_layer)[0]
                if live(t - 4) and layer_y == 0:
                    transpose_y(t - 4, r, loop_layer)
                if now:
                    scores(t, r, 1, masked)
                if last:
                    scoresT(t - 2, r2, 6, masked)
                if live(t - 3):
                    transpose_attn(t - 3)
                if now:
                    scores(t, r, 2, masked)
                if last:
                    scoresT(t - 2, r2, 7, masked)
                    transpose_o(t - 2, 0)
                if now:
                    scores(t, r, 3, masked)
                if before:
                    scoresT(t - 1, r1, 0, masked)
                if live(t - 3):
                    project_out(t - 3, place(t - 3, loop_layer)[0])
                if now:
                    scores(t, r, 4, masked)
                if before:
                    scoresT(t - 1, r1, 1, masked)
                if ahead:
                    project_qk(t + 2, ra, layer_ahead, b_ahead)
                if now:
                    scores(t, r, 5, masked)
                if before:
                    scoresT(t - 1, r1, 2, masked)
                if last:
                    probs_v(t - 2, r2, 1)
                if now:
                    scores(t, r, 6, masked)
                if before:
                    scoresT(t - 1, r1, 3, masked)
                if ahead and layer_ahead == 0:
                    project_v(t + 2, ra)
                if now:
                    scores(t, r, 7, masked)
                if before:
                    scoresT(t - 1, r1, 4, masked)
                if last:
                    transpose_o(t - 2, 1)
                if now:
                    transpose_max(t, r, loop_layer)

            pe.wait_ge(ident_step, 6)
            for t in range(FIRST_PHASE, 0):
                phase(0, t, None, False)
            pe.wait_ge(flag_ready, 1)
            any_mask = pe.value_load(mask_flag[0:1, 0:1])
            with pe.If(any_mask):
                walk(pe, lambda turn, step, layer: phase(turn, step, layer, True), 0)
            with pe.Else():
                walk(pe, lambda turn, step, layer: phase(turn, step, layer, False), 0)


def kernel(**inputs):
    import concourse.bacc as bacc
    from concourse.bass_utils import run_bass_kernel_spmd

    def both(name):
        return [np.asarray(inputs[f"L{n}_xattn_{name}"]) for n in range(LAYERS)]

    q_order = np.arange(D).reshape(HEADS // 2, 2, HD).transpose(1, 2, 0).reshape(-1)
    k_order = np.arange(KVD).reshape(KV, HD).T.reshape(-1)
    o_order = np.arange(D).reshape(2, HALF, GROUP, HD).transpose(0, 2, 1, 3).reshape(-1)
    x, context = np.asarray(inputs["x"]), np.asarray(inputs["ctx_2048"])
    arrays = {
        "x": x,
        "xT": x.transpose(2, 0, 1),
        "ctxT": context.transpose(0, 2, 1),
        "mask": np.asarray(inputs["mask_Bx1xSxS2_ff0"]),
        "w_q": np.stack([w[:, q_order] for w in both("Wq")]),
        "w_kv": np.concatenate([w[:, k_order] for w in both("Wk")] + both("Wv"), axis=1),
        "w_o": np.stack([w[o_order] for w in both("Wo")]),
        "b_q": np.stack([b[q_order].reshape(KT, P) for b in both("bq")]).transpose(2, 0, 1),
        "b_k": np.concatenate([b[k_order] for b in both("bk")])[:, None],
        "rows": np.stack([np.concatenate(r) for r in zip(both("bo"), both("gamma"), both("beta"), both("bv"))]),
    }
    arrays["rows"] = arrays["rows"].reshape(-1)
    nc = bacc.Bacc("TRN2", target_bir_lowering=False, num_devices=1)
    arrays = {name: np.ascontiguousarray(a) for name, a in arrays.items()}
    args = [nc.dram_tensor(name, a.shape, mybir.dt.from_np(a.dtype), kind="ExternalInput").ap()
            for name, a in arrays.items()]
    result = nc.dram_tensor("result", (BATCH, L, D), F32, kind="ExternalOutput").ap()
    cross_attention(nc, *args, result)
    done = run_bass_kernel_spmd(nc, [arrays], core_ids=[0])
    return done.results[0]["result"]
```

```python
from contextlib import ExitStack

import concourse.bass as bass
import numpy as np
from concourse import mybir

F32 = mybir.dt.float32
BF16 = mybir.dt.bfloat16
I32 = mybir.dt.int32
ALU = mybir.AluOpType
ACT = mybir.ActivationFunctionType
AX = mybir.AxisListType

P = 128
LAYERS, BATCH, L, S, D = 2, 16, 128, 128, 256
HEADS, KV, HD = 32, 8, 8
GROUP = HEADS // KV
KT = D // P
UNITS = LAYERS * BATCH
PARTS = 3
TERM_ROWS = PARTS * PARTS * HD
SCORE_ROWS = 96
MAX_ROW = 96
STACK_ROWS = MAX_ROW + PARTS
RING = 4
HALF = KV // 2
KVD = KV * HD
SCALE = float(HD) ** -0.5
EPS = 1e-6
TWO_ONES = float(np.array([0x3F803F80], np.uint32).view(np.float32)[0])
LOOPS = ((0, 4, 12), (1, 20, 28))
FIRST_PHASE, LAST_PHASE = -2, UNITS + 3


def live(u):
    return not isinstance(u, int) or 0 <= u < UNITS


def place(u, layer):
    return (u // BATCH, u % BATCH) if isinstance(u, int) else (layer, u - BATCH * layer)


def total(n, first, second, layer):
    if not isinstance(n, int):
        return n * first if layer == 0 else n * second + BATCH * (first - second)
    return first * min(n, BATCH) + second * max(n - BATCH, 0)


def need(engine, sem, count):
    if not isinstance(count, int) or count > 0:
        engine.wait_ge(sem, count)


def upto(u):
    return min(u, UNITS - 1) if isinstance(u, int) else u


def walk(engine, phase, first=FIRST_PHASE):
    for layer, start, end in LOOPS:
        for t in range(first, start + 1):
            phase(0, t, None)
        with engine.Fori(start, end - RING + 1, RING) as turn:
            for step in range(1, RING + 1):
                phase(turn, step, layer)
        first = end + 1
    for t in range(first, LAST_PHASE + 1):
        phase(0, t, None)


def cross_attention(nc, x, xT, ctxT, mask, w_q, w_kv, w_o, b_q, b_k, rows, out):
    with ExitStack() as ctx:
        def sb(name, shape, dt):
            return ctx.enter_context(nc.sbuf_tensor(name, shape, dt))

        def sem(name):
            return ctx.enter_context(nc.semaphore(name))

        q_scratch = nc.dram_tensor("q_scratch", (UNITS, PARTS, P, KT * L), BF16).ap()
        k_scratch = nc.dram_tensor("k_scratch", (BATCH, PARTS, LAYERS * KVD, S), BF16).ap()

        x_sb = sb("x_sb", [P, BATCH, D], F32)
        xT_sb = sb("xT_sb", [P, KT, BATCH, L], F32)
        ctx_sb = sb("ctx_sb", [P, RING, KT, S], F32)
        mask_sb = sb("mask_sb", [P, BATCH, S], F32)
        mask_parts = sb("mask_parts", [P, RING, PARTS, S], BF16)
        wq_sb = sb("wq_sb", [P, LAYERS, KT, D], F32)
        wkv_sb = sb("wkv_sb", [P, KT, 2, LAYERS * KVD], F32)
        wo_sb = sb("wo_sb", [P, LAYERS, KT, D], F32)
        bq_sb = sb("bq_sb", [P, LAYERS, KT], F32)
        bq_scaled = sb("bq_scaled", [P, LAYERS, KT], F32)
        bk_sb = sb("bk_sb", [LAYERS * KVD, 1], F32)
        rows_sb = sb("rows_sb", [P, LAYERS, 3 * D + KVD], F32)
        identf = sb("identf", [P, P], F32)
        ident = sb("ident", [P, P], BF16)
        qT = sb("qT", [P, KT * L], F32)
        kT = sb("kT", [P, S], F32)
        q_rest = sb("q_rest", [P, KT * L], F32)
        k_rest = sb("k_rest", [P, S], F32)
        mask_now = sb("mask_now", [P, S], F32)
        zeros = sb("zeros", [P, S], F32)
        held = sb("held", [P, RING], F32)
        held_v = sb("held_v", [P, 1], F32)
        m_rest = sb("m_rest", [P, S], F32)
        q_parts = sb("q_parts", [P, 2, PARTS, KT * L], BF16)
        k_parts = sb("k_parts", [P, 2, PARTS, S], BF16)
        q_stack = sb("q_stack", [P, RING, HEADS, L], BF16)
        k_stack = sb("k_stack", [P, RING, KV, S], BF16)
        row_max = sb("row_max", [P, 2, PARTS * HEADS], F32)
        max_rest = sb("max_rest", [PARTS * HEADS, L], F32)
        max_parts = sb("max_parts", [PARTS * HEADS, 2, L], BF16)
        v_ones = sb("v_ones", [P, RING, KV, 32], F32)
        v_next = sb("v_next", [P, BATCH, KVD], F32)
        probs = sb("probs", [P, 2, KV, GROUP * L], F32)
        oT_sb = sb("oT_sb", [P, 2, GROUP * L], F32)
        recip = sb("recip", [P, 2, 16], F32)
        attn = sb("attn", [P, D], F32)
        attnT = sb("attnT", [P, KT, L], F32)
        x_bo = sb("x_bo", [P, D], F32)
        z = sb("z", [P, D], F32)
        stats = sb("stats", [P, 6], F32)
        mean_var = sb("mean_var", [P, 2], F32)
        var_eps = sb("var_eps", [P, 1], F32)
        minus_half = sb("minus_half", [P, 1], F32)
        rstd = sb("rstd", [P, 1], F32)
        normed = sb("normed", [P, D], F32)
        scaled = sb("scaled", [P, D], F32)
        y = sb("y", [P, 2, D], F32)
        mask_top = sb("mask_top", [P, 1], F32)
        mask_any = sb("mask_any", [P, 1], F32)
        mask_flag = sb("mask_flag", [P, 1], I32)

        def bank(name):
            return ctx.enter_context(nc.psum_tensor(name, [P, 512], F32))

        s_bank = [bank("s_bank0"), bank("s_bank1")]
        t_bank = [bank("t_bank0"), bank("t_bank1")]
        oT_bank = bank("oT_bank")
        o_bank = bank("o_bank")
        qk_bank = bank("qk_bank")
        misc_bank = bank("misc_bank")

        weights_loaded = sem("weights_loaded")
        biases_loaded = sem("biases_loaded")
        rows_loaded = sem("rows_loaded")
        later_weights_loaded = sem("later_weights_loaded")
        x_loaded = sem("x_loaded")
        all_masks_loaded = sem("all_masks_loaded")
        inputs_loaded = sem("inputs_loaded")
        ident_step = sem("ident_step")
        pad_step = sem("pad_step")
        q_padded = sem("q_padded")
        k_padded = sem("k_padded")
        bias_scaled = sem("bias_scaled")
        flag_step = sem("flag_step")
        flag_ready = sem("flag_ready")
        mask_step = sem("mask_step")
        qk_projected = sem("qk_projected")
        v_projected = sem("v_projected")
        qk_read = sem("qk_read")
        v_ready = sem("v_ready")
        v_next_ready = sem("v_next_ready")
        q_split = sem("q_split")
        k_split = sem("k_split")
        q_stored = sem("q_stored")
        k_stored = sem("k_stored")
        stacks_loaded = sem("stacks_loaded")
        scores_ready = sem("scores_ready")
        max_done = sem("max_done")
        max_copied = sem("max_copied")
        maxT_ready = sem("maxT_ready")
        maxT_step = sem("maxT_step")
        max_rows_loaded = sem("max_rows_loaded")
        scoresT_ready = sem("scoresT_ready")
        exp_done = sem("exp_done")
        oT_ready = sem("oT_ready")
        oT_copied = sem("oT_copied")
        o_ready = sem("o_ready")
        recip_done = sem("recip_done")
        o_normed = sem("o_normed")
        attnT_ready = sem("attnT_ready")
        attnT_copied = sem("attnT_copied")
        proj_ready = sem("proj_ready")
        x_bo_ready = sem("x_bo_ready")
        rstd_ready = sem("rstd_ready")
        norm_step = sem("norm_step")
        affine_step = sem("affine_step")
        yT_ready = sem("yT_ready")
        yT_copied = sem("yT_copied")
        y_left = sem("y_left")

        MAXT_STEPS, NORM_STEPS, MASK_STEPS = 4, 5, 5
        QK_READS = (6, 4)
        STACK_DMAS = 4
        INPUT_DMAS = 2
        DVE_SPLITS = 1

        def split(engine, f, rest, parts, step, done):
            engine.tensor_tensor(rest, f, parts[0], ALU.subtract).then_inc(step, 1)
            engine.tensor_tensor(parts[1], f, parts[0], ALU.subtract).then_inc(step, 1)
            engine.wait_ge(step, done + 2)
            engine.tensor_tensor(parts[2], rest, parts[1], ALU.subtract).then_inc(step, 1)

        def split_qk(engine, u, ru, layer):
            need(engine, qk_read, total(u, *QK_READS, layer) + 4)
            split(engine, qT[:], q_rest[:], [q_parts[:, ru % 2, n] for n in range(PARTS)], q_split, 3 * u)
            if place(u, layer)[0] == 0:
                need(engine, qk_read, total(u + 1, *QK_READS, layer))
                split(engine, kT[:], k_rest[:], [k_parts[:, ru % 2, n] for n in range(PARTS)], k_split, 3 * u)

        block = ctx.enter_context(nc.Block())

        @block.sync
        def _(sp):
            xT_d = xT.rearrange("(k p) b l -> p k b l", p=P)

            def load_inputs(b, slot, loaded):
                for to, from_ in ((xT_sb[:, :, b], xT_d[:, :, b]),
                                  (ctx_sb[:, slot], ctxT[b].rearrange("(k p) s -> p k s", p=P))):
                    sp.dma_start(to, from_).then_inc(loaded, 16)

            STARTERS = 2
            sp.dma_start(wq_sb[:, 0], w_q[0].rearrange("(k p) n -> p k n", p=P)).then_inc(weights_loaded, 16)
            load_inputs(0, 0, weights_loaded)
            sp.dma_start(wkv_sb[:].rearrange("p k a n -> p k (a n)"),
                         w_kv.rearrange("(k p) n -> p k n", p=P)).then_inc(weights_loaded, 16)
            sp.dma_start(bq_sb[:], b_q).then_inc(biases_loaded, 16)
            sp.dma_start(bk_sb[:], b_k).then_inc(biases_loaded, 16)
            load_inputs(1, 1, inputs_loaded)
            sp.dma_start(rows_sb[:].rearrange("p a n -> p (a n)"), rows.partition_broadcast(P)).then_inc(rows_loaded, 16)
            sp.dma_start(mask_sb[:], mask.rearrange("b o l s -> l (b o) s")).then_inc(all_masks_loaded, 16)

            def phase(turn, step, loop_layer):
                t, r = turn + step, step % RING

                def of(per, k):
                    return turn * per + per * (step + k)

                if not isinstance(turn, int):
                    for count in (of(MAXT_STEPS, 0), of(16, -1), of(KV, -RING), of(3, 3), of(1, 0),
                                  of(16 * INPUT_DMAS, 2), of(16, 0), of(2, -3), of(16, -4), of(1, -3),
                                  of(16 * STACK_DMAS, 2), of(16, 3), of(KV, 3 - RING)):
                        sp.to_reg(count)
                if live(t - 1):
                    need(sp, maxT_step, of(MAXT_STEPS, 0))
                    need(sp, max_rows_loaded, of(16, -1))
                    need(sp, scoresT_ready, of(KV, -RING))
                    sp.dma_start(q_stack[MAX_ROW:MAX_ROW + PARTS, (r - 1) % RING],
                                 max_parts[:, (r - 1) % 2].rearrange("p (o l) -> p o l", o=1)).then_inc(max_rows_loaded, 16)
                u, ru = t - 4, r
                if live(u):
                    layer, b = place(u, loop_layer)
                    need(sp, affine_step, of(2, -3))
                    need(sp, y_left, of(16, -4))
                    if layer == LAYERS - 1:
                        sp.dma_start(out[b], y[:, ru % 2]).then_inc(y_left, 16)
                    else:
                        need(sp, x_bo_ready, of(1, -3))
                        sp.dma_start(x_sb[:, b], y[:, ru % 2]).then_inc(y_left, 16)
                layer, b = place(t + 3, loop_layer)
                if (not isinstance(t, int) or t + 3 >= STARTERS) and layer == 0:
                    need(sp, qk_projected, of(1, 0))
                    need(sp, v_projected, of(1, 0))
                    need(sp, inputs_loaded, of(16 * INPUT_DMAS, 2))
                    load_inputs(b, (r + 3) % RING, inputs_loaded)
                layer, b = place(t, loop_layer)
                if live(t) and layer == 0:
                    need(sp, x_loaded, of(16, 0))
                    sp.dma_start(x_sb[:, b], x[b]).then_inc(x_loaded, 16)
                u, ru = t + 2, (r + 2) % RING
                layer, b = place(u, loop_layer)
                if live(u):
                    need(sp, q_split, of(3, 3))
                    sp.dma_start(q_scratch[u].rearrange("a p n -> p a n"), q_parts[:, ru % 2]).then_inc(q_stored, 16)
                    if layer == 0:
                        need(sp, k_split, of(3, 3))
                        sp.dma_start(k_scratch[b].rearrange("a p n -> p a n"), k_parts[:, ru % 2]
                                     ).then_inc(k_stored, 16)
                    need(sp, stacks_loaded, of(16 * STACK_DMAS, 2))
                    need(sp, scoresT_ready, of(KV, 3 - RING))
                    if isinstance(u, int) and u < RING:
                        need(sp, k_padded, 1)
                        need(sp, q_padded, u + 1)
                    need(sp, q_stored, of(16, 3))
                    sp.dma_start(q_stack[0:TERM_ROWS, ru].rearrange("p h l -> p (h l)"),
                                 q_scratch[u].rearrange("a (d h) n -> (a d) (h n)", d=HD).partition_broadcast(PARTS)
                                 ).then_inc(stacks_loaded, 16)
                    if layer == 0:
                        need(sp, k_stored, of(16, 3))
                    for part in range(PARTS):
                        first = part * PARTS * HD
                        k_rows = k_scratch[b, part, layer * KVD:(layer + 1) * KVD].rearrange("(d h) n -> d (h n)", d=HD)
                        sp.dma_start(k_stack[first:first + PARTS * HD, ru].rearrange("p h l -> p (h l)"),
                                     k_rows.partition_broadcast(PARTS)).then_inc(stacks_loaded, 16)
                if isinstance(t, int) and t == 0:
                    sp.dma_start(wo_sb[:], w_o.rearrange("a (k p) n -> p a k n", p=P)).then_inc(later_weights_loaded, 16)
                    sp.dma_start(wq_sb[:, 1], w_q[1].rearrange("(k p) n -> p k n", p=P)).then_inc(later_weights_loaded, 16)

            walk(sp, phase)
            sp.wait_ge(y_left, 16 * UNITS)
            sp.wait_ge(q_stored, 16 * UNITS)
            sp.wait_ge(k_stored, 16 * BATCH)

        @block.gpsimd
        def _(pool):
            nc.gpsimd.memset(identf[:], 0.0).then_inc(ident_step, 1)
            nc.gpsimd.memset(ident[:], 0.0).then_inc(ident_step, 1)
            pool.wait_ge(ident_step, 2)
            nc.gpsimd.memset(zeros[:], 0.0).then_inc(ident_step, 1)
            nc.gpsimd.memset(minus_half[:], -0.5).then_inc(ident_step, 1)
            for m in (identf, ident):
                nc.gpsimd.affine_select(out=m[:], in_=m[:], compare_op=ALU.not_equal, fill=1.0, base=0,
                                        pattern=[[-1, P]], channel_multiplier=1).then_inc(ident_step, 1)

            for slot in range(RING):
                if slot == 0:
                    pool.wait_ge(ident_step, 6)
                else:
                    pool.wait_ge(q_padded, slot)
                nc.gpsimd.memset(q_stack[64:MAX_ROW, slot].rearrange("p h l -> p (h l)").bitcast(F32), 0.0
                                 ).then_inc(q_padded, 1)

            def flags():
                pool.wait_ge(flag_step, 1)
                nc.gpsimd.partition_all_reduce(mask_any[:], mask_top[:], P, bass.bass_isa.ReduceOp.max).then_inc(flag_step, 1)

            def hold(n):
                nc.gpsimd.tensor_tensor(held[:, n:n + 1], minus_half[:], minus_half[:], ALU.add)

            def phase(turn, step, loop_layer):
                t, r = turn + step, step % RING
                u, ru = t + 2, (r + 2) % RING
                if live(u) and not (isinstance(u, int) and u < DVE_SPLITS):
                    split_qk(pool, u, ru, loop_layer)
                u = t - 3
                if live(u):
                    layer, b = place(u, loop_layer)
                    need(pool, norm_step, NORM_STEPS * u + 4)
                    nc.gpsimd.tensor_tensor(rstd[:], var_eps[:], minus_half[:], ALU.pow).then_inc(rstd_ready, 1)
                    need(pool, norm_step, NORM_STEPS * (u + 1))
                    need(pool, affine_step, 2 * u)
                    nc.gpsimd.tensor_tensor(scaled[:], normed[:], rows_sb[:, layer, D:2 * D],
                                            ALU.mult).then_inc(affine_step, 1)
                    if not isinstance(u, int) and layer == 0 or isinstance(u, int) and u - 2 < BATCH:
                        need(pool, yT_ready, u - 1)
                    need(pool, y_left, 16 * (u - 1))
                    pool.wait_ge(affine_step, 2 * u + 1)
                    nc.gpsimd.tensor_tensor(y[:, (r - 3) % 2], scaled[:], rows_sb[:, layer, 2 * D:3 * D],
                                            ALU.add).then_inc(affine_step, 1)
                u, ru = t + 1, (r + 1) % RING
                if live(u):
                    layer, b = place(u, loop_layer)
                    need(pool, scoresT_ready, KV * (u - RING + 1))
                    need(pool, mask_step, MASK_STEPS * u)
                    hold(step % RING)
                    parts = [mask_parts[:, ru, n] for n in range(PARTS)]
                    for copy in (mask_now[:], parts[0]):
                        nc.gpsimd.tensor_tensor(copy, mask_sb[:, b], zeros[:], ALU.add).then_inc(mask_step, 1)
                    pool.wait_ge(mask_step, MASK_STEPS * u + 2)
                    split(pool, mask_now[:], m_rest[:], parts, mask_step, MASK_STEPS * u + 2)
                u = t - 2
                if live(u):
                    layer, b = place(u, loop_layer)
                    if isinstance(u, int) and u == 0:
                        pool.wait_ge(rows_loaded, 16)
                    if layer == 0:
                        need(pool, x_loaded, 16 * (u + 1))
                    need(pool, norm_step, NORM_STEPS * (u - 1) + 1)
                    hold(step % RING)
                    nc.gpsimd.tensor_tensor(x_bo[:], x_sb[:, b], rows_sb[:, layer, 0:D], ALU.add).then_inc(x_bo_ready, 1)

            pool.wait_ge(q_padded, RING)
            phase(0, FIRST_PHASE, None)
            flags()
            walk(pool, phase, FIRST_PHASE + 1)

        @block.scalar
        def _(act):
            def exp(u, ru, kv):
                need(act, scoresT_ready, KV * u + kv + 1)
                need(act, oT_ready, 2 * (u - 2) + kv // HALF + 1)
                nc.scalar.activation(probs[:, ru % 2, kv], t_bank[kv % 2][:], ACT.Exp).then_inc(exp_done, 1)

            def copy_oT(u, ru, half):
                need(act, oT_ready, 2 * u + half + 1)
                need(act, o_ready, 2 * (u - 1) + half + 1)
                nc.scalar.activation(oT_sb[:, half], oT_bank[:], ACT.Copy).then_inc(oT_copied, 1)

            def read_q(u, ru, layer, k):
                if k == 0:
                    need(act, qk_projected, u + 1)
                    need(act, q_split, 3 * u)
                    need(act, k_split, 3 * u if place(u, layer)[0] == 0 else 0)
                    need(act, q_stored, 16 * (u - 1))
                    need(act, k_stored, 16 * (u - 1) if place(u, layer)[0] == 0 else 0)
                for q in (qT[:, k * L:(k + 1) * L], q_parts[:, ru % 2, 0, k * L:(k + 1) * L]):
                    nc.scalar.activation(q, qk_bank[:, k * L:(k + 1) * L], ACT.Identity,
                                         bias=bq_scaled[:, place(u, layer)[0], k:k + 1], scale=SCALE).then_inc(qk_read, 1)

            def phase(turn, step, loop_layer):
                t, r = turn + step, step % RING
                r1, r2, ra = (r - 1) % RING, (r - 2) % RING, (r + 2) % RING
                before, last, ahead = live(t - 1), live(t - 2), live(t + 2)
                if last:
                    exp(t - 2, r2, 4)
                if ahead:
                    read_q(t + 2, ra, loop_layer, 0)
                if live(t - 3):
                    need(act, attnT_ready, t - 2)
                    need(act, proj_ready, t - 3)
                    nc.scalar.activation(attnT[:], o_bank[:, 0:D].rearrange("p (k l) -> p k l", k=KT),
                                         ACT.Copy).then_inc(attnT_copied, 1)
                if ahead:
                    read_q(t + 2, ra, loop_layer, 1)
                if last:
                    exp(t - 2, r2, 5)
                if ahead and place(t + 2, loop_layer)[0] == 0:
                    for kk in (kT[:], k_parts[:, ra % 2, 0]):
                        nc.scalar.activation(kk, qk_bank[:, D:D + S], ACT.Identity, bias=bk_sb[:, 0:1]).then_inc(qk_read, 1)
                if last:
                    copy_oT(t - 2, r2, 0)
                    exp(t - 2, r2, 6)
                    exp(t - 2, r2, 7)
                layer, b = place(t - 4, loop_layer)
                if live(t - 4) and layer == 0:
                    need(act, yT_ready, t - 3)
                    nc.scalar.activation(xT_sb[:, :, b], qk_bank[:, 0:KT * L].rearrange("p (k l) -> p k l", k=KT),
                                         ACT.Copy).then_inc(yT_copied, 1)
                if before:
                    exp(t - 1, r1, 0)
                    exp(t - 1, r1, 1)
                if last:
                    copy_oT(t - 2, r2, 1)
                if before:
                    exp(t - 1, r1, 2)
                    exp(t - 1, r1, 3)

            act.wait_ge(biases_loaded, 32)
            nc.scalar.activation(bq_scaled[:], bq_sb[:], ACT.Copy, scale=SCALE).then_inc(bias_scaled, 1)
            act.wait_ge(bias_scaled, 1)
            walk(act, phase)

        @block.vector
        def _(dve):
            def words(rows):
                return rows.rearrange("p r h l -> p (r h l)").bitcast(F32)

            nc.vector.memset(words(k_stack[64:MAX_ROW]), 0.0).then_inc(pad_step, 1)
            nc.vector.memset(words(k_stack[MAX_ROW:P]), TWO_ONES).then_inc(pad_step, 1)
            nc.vector.memset(v_ones[:], 1.0).then_inc(pad_step, 1)
            dve.wait_ge(pad_step, 3)
            nc.vector.memset(recip[:], 0.0).then_inc(k_padded, 1)

            def flags():
                dve.wait_ge(all_masks_loaded, 16)
                nc.vector.tensor_reduce(mask_top[:], mask_sb[:], AX.XY, ALU.max,
                                        apply_absolute_value=True).then_inc(flag_step, 1)
                dve.wait_ge(flag_step, 2)
                nc.vector.tensor_scalar(mask_flag[:], mask_any[:], 0.0, None, ALU.not_equal).then_inc(flag_ready, 1)

            def maximum(u, ru, kv):
                need(dve, scores_ready, KV * u + kv + 1)
                need(dve, maxT_ready, u - 1)
                nc.vector.tensor_reduce(row_max[:, ru % 2, GROUP * kv:GROUP * (kv + 1)],
                                        s_bank[kv % 2][:].rearrange("p (g s) -> p g s", g=GROUP),
                                        AX.X, ALU.max).then_inc(max_done, 1)

            def copy_max(u, ru):
                dve.wait_ge(max_done, KV * (u + 1))
                nc.vector.tensor_copy(row_max[:, ru % 2, HEADS:].rearrange("p (c h) -> p c h", h=HEADS),
                                      row_max[:, ru % 2, 0:HEADS].unsqueeze(1).broadcast_to([P, PARTS - 1, HEADS])
                                      ).then_inc(max_copied, 1)

            def max_rows(u, ru):
                m, parts = misc_bank[0:PARTS * HEADS, 0:L], max_parts[:, ru % 2]
                need(dve, maxT_ready, u + 1)
                need(dve, max_rows_loaded, 16 * (u - 1))
                nc.vector.tensor_scalar(parts, m, -1.0, None, ALU.mult).then_inc(maxT_step, 1)
                dve.wait_ge(maxT_step, MAXT_STEPS * u + 1)
                nc.vector.scalar_tensor_tensor(out=max_rest[:], in0=m, scalar=-1.0, in1=parts,
                                               op0=ALU.mult, op1=ALU.subtract).then_inc(maxT_step, 1)
                dve.wait_ge(maxT_step, MAXT_STEPS * u + 2)
                nc.vector.tensor_copy(parts[0:2 * HEADS], max_rest[0:2 * HEADS]).then_inc(maxT_step, 1)
                dve.wait_ge(maxT_step, MAXT_STEPS * u + 3)
                nc.vector.tensor_tensor(parts[0:HEADS], max_rest[0:HEADS], parts[0:HEADS], ALU.subtract
                                        ).then_inc(maxT_step, 1)

            def sums(u, half):
                need(dve, o_ready, 2 * u + half + 1)
                nc.vector.reciprocal(recip[:, half], o_bank[:].rearrange("p (n c) -> p n c", c=32)[:, :, HD]
                                     ).then_inc(recip_done, 1)

            def normalise(u, half):
                o = o_bank[:].rearrange("p (n c) -> p n c", c=32)
                dve.wait_ge(recip_done, 2 * u + half + 1)
                need(dve, attnT_ready, u)
                nc.vector.tensor_tensor(attn[:, half * P:(half + 1) * P].rearrange("p (n c) -> p n c", c=HD),
                                        o[:, :, 0:HD], recip[:, half].unsqueeze(2).broadcast_to([P, 16, HD]),
                                        ALU.mult).then_inc(o_normed, 1)

            def norm(u, part):
                done = NORM_STEPS * u + part
                if part == 0:
                    need(dve, proj_ready, u + 1)
                    need(dve, x_bo_ready, u + 1)
                    nc.vector.tensor_tensor(z[:], misc_bank[:, 0:D], x_bo[:], ALU.add).then_inc(norm_step, 1)
                if part == 1:
                    dve.wait_ge(norm_step, done)
                    nc.vector.bn_stats(stats[:], z[:]).then_inc(norm_step, 1)
                if part == 2:
                    dve.wait_ge(norm_step, done)
                    nc.vector.memset(held_v[:], 0.0)
                    nc.vector.bn_aggr(mean_var[:], stats[:]).then_inc(norm_step, 1)
                if part == 3:
                    dve.wait_ge(norm_step, done)
                    nc.vector.tensor_scalar(var_eps[:], mean_var[:, 1:2], EPS, None, ALU.add).then_inc(norm_step, 1)
                if part == 4:
                    need(dve, rstd_ready, u + 1)
                    need(dve, affine_step, 2 * u - 1)
                    nc.vector.tensor_scalar(normed[:], z[:], mean_var[:, 0:1], rstd[:, 0:1],
                                            ALU.subtract, ALU.mult).then_inc(norm_step, 1)

            def values(u, ru, layer, b):
                def heads(v):
                    return v.rearrange("p (h d) -> p h d", d=HD)

                need(dve, oT_ready, 2 * (u - RING + 1))
                if layer == 0:
                    need(dve, v_projected, u + 1)
                    bias = rows_sb[:, :, 3 * D:3 * D + KVD]
                    nc.vector.tensor_tensor(v_next[:, b], misc_bank[:, KVD:2 * KVD], bias[:, 1], ALU.add
                                            ).then_inc(v_next_ready, 1)
                    nc.vector.tensor_tensor(v_ones[:, ru, :, 0:HD], heads(misc_bank[:, 0:KVD]), heads(bias[:, 0]), ALU.add
                                            ).then_inc(v_ready, 1)
                else:
                    if isinstance(u, int) and u == BATCH:
                        need(dve, v_next_ready, BATCH)
                    nc.vector.tensor_copy(v_ones[:, ru, :, 0:HD], heads(v_next[:, b])).then_inc(v_ready, 1)

            def phase(turn, step, loop_layer):
                t, r = turn + step, step % RING
                now, before, last, norming = live(t), live(t - 1), live(t - 2), live(t - 3)
                if norming:
                    sums(t - 3, 1)
                    normalise(t - 3, 1)
                if now:
                    maximum(t, r, 0)
                if before:
                    max_rows(t - 1, (r - 1) % RING)
                if now:
                    maximum(t, r, 1)
                    maximum(t, r, 2)
                if norming:
                    norm(t - 3, 0)
                if now:
                    maximum(t, r, 3)
                if norming:
                    norm(t - 3, 1)
                if last:
                    sums(t - 2, 0)
                if norming:
                    norm(t - 3, 2)
                if last:
                    normalise(t - 2, 0)
                if norming:
                    norm(t - 3, 3)
                if now:
                    maximum(t, r, 4)
                    maximum(t, r, 5)
                if norming:
                    norm(t - 3, 4)
                if now:
                    maximum(t, r, 6)
                if live(t + 2):
                    values(t + 2, (r + 2) % RING, *place(t + 2, loop_layer))
                if now:
                    maximum(t, r, 7)
                    copy_max(t, r)

            dve.wait_ge(k_padded, 1)
            for u in range(DVE_SPLITS):
                split_qk(dve, u, u, None)
            dve.wait_ge(rows_loaded, 16)
            phase(0, FIRST_PHASE, None)
            flags()
            walk(dve, phase, FIRST_PHASE + 1)

        @block.tensor
        def _(pe):
            def scores(u, ru, kv, masked):
                if kv == 0:
                    if isinstance(u, int) and u < RING:
                        pe.wait_ge(q_padded, u + 1)
                    need(pe, stacks_loaded, 16 * STACK_DMAS * (u + 1))
                    if masked:
                        need(pe, mask_step, MASK_STEPS * (u + 1))
                need(pe, max_done, KV * u + kv - 1)
                for g in range(GROUP):
                    mm = nc.tensor.matmul(s_bank[kv % 2][:, g * S:(g + 1) * S],
                                          q_stack[0:SCORE_ROWS, ru, GROUP * kv + g], k_stack[0:SCORE_ROWS, ru, kv],
                                          start=(g == 0), stop=(g == GROUP - 1 and not masked), skip_group_check=True)
                if masked:
                    for n in range(PARTS):
                        mm = nc.tensor.matmul(s_bank[kv % 2][:].rearrange("p (g s) -> p g s", g=GROUP), ident[:],
                                              mask_parts[:, ru, n:n + 1].broadcast_to([P, GROUP, S]),
                                              start=False, stop=(n == PARTS - 1), skip_group_check=True)
                mm.then_inc(scores_ready, 1)

            def scoresT(u, ru, kv, masked):
                if kv == 0:
                    need(pe, max_rows_loaded, 16 * (u + 1))
                need(pe, exp_done, KV * u + kv - 1)
                mm = nc.tensor.matmul(t_bank[kv % 2][:], k_stack[0:STACK_ROWS, ru, kv],
                                      q_stack[0:STACK_ROWS, ru, GROUP * kv:GROUP * (kv + 1)],
                                      start=True, stop=not masked)
                if masked:
                    for n in range(PARTS):
                        mm = nc.tensor.matmul(t_bank[kv % 2][:].rearrange("p (g l) -> p g l", g=GROUP),
                                              mask_parts[:, ru, n], ident[:].unsqueeze(1).broadcast_to([P, GROUP, L]),
                                              start=False, stop=(n == PARTS - 1))
                mm.then_inc(scoresT_ready, 1)

            def project_v(u, ru):
                if not isinstance(u, int) or u >= 5:
                    need(pe, norm_step, NORM_STEPS * (u - 5) + 1)
                elif u >= 3:
                    need(pe, maxT_step, MAXT_STEPS * (u - 3) + 2)
                else:
                    need(pe, v_ready, u)
                for k in range(KT):
                    mm = nc.tensor.matmul(misc_bank[:, 0:LAYERS * KVD], ctx_sb[:, ru, k], wkv_sb[:, k, 1],
                                          start=(k == 0), stop=(k == KT - 1))
                mm.then_inc(v_projected, 1)

            def project_qk(u, ru, layer, b):
                if isinstance(u, int):
                    need(pe, yT_copied, min(u - 6, BATCH))
                    need(pe, qk_read, total(u, *QK_READS, None))
                elif layer == 0:
                    need(pe, yT_copied, u - 6)
                else:
                    need(pe, qk_read, total(u, *QK_READS, layer))
                if isinstance(u, int) and u == 0:
                    pe.wait_ge(weights_loaded, 64)
                if isinstance(u, int) and u == BATCH:
                    pe.wait_ge(later_weights_loaded, 32)
                if layer == 0:
                    need(pe, inputs_loaded, 16 * INPUT_DMAS * u)
                for n in range(KT):
                    for k in range(KT):
                        mm = nc.tensor.matmul(qk_bank[:, n * L:(n + 1) * L], wq_sb[:, layer, k, n * P:(n + 1) * P],
                                              xT_sb[:, k, b],
                                              start=(n == 0 and k == 0), stop=(k == KT - 1), skip_group_check=True)
                if layer == 0:
                    for k in range(KT):
                        mm = nc.tensor.matmul(qk_bank[:, D:D + S], wkv_sb[:, k, 0], ctx_sb[:, ru, k],
                                              start=False, stop=(k == KT - 1), skip_group_check=True)
                mm.then_inc(qk_projected, 1)

            def transpose_max(u, ru, layer):
                need(pe, max_copied, u + 1)
                if not isinstance(u, int) and layer == 0 or isinstance(u, int) and u + 2 < BATCH:
                    need(pe, v_ready, u + 3)
                else:
                    need(pe, norm_step, NORM_STEPS * (u - 3) + 1)
                nc.tensor.transpose(misc_bank[0:PARTS * HEADS, 0:L], row_max[:, ru % 2],
                                    identf[:]).then_inc(maxT_ready, 1)

            def probs_v(u, ru, half):
                need(pe, exp_done, KV * u + HALF * (half + 1))
                need(pe, oT_copied, 2 * u + half)
                for j in range(HALF):
                    kv = half * HALF + j
                    mm = nc.tensor.matmul(oT_bank[32 * j:32 * (j + 1)], v_ones[:, ru, kv], probs[:, ru % 2, kv],
                                          start=True, stop=True)
                mm.then_inc(oT_ready, 1)

            def transpose_o(u, half):
                need(pe, oT_copied, 2 * u + half + 1)
                if half == 1:
                    need(pe, o_normed, 2 * u + 1)
                else:
                    need(pe, attnT_copied, u)
                for g in range(GROUP):
                    mm = nc.tensor.transpose(o_bank[:, g * P:(g + 1) * P], oT_sb[:, half, g * L:(g + 1) * L], identf[:])
                mm.then_inc(o_ready, 1)

            def transpose_attn(u):
                need(pe, o_normed, 2 * (u + 1))
                for k in range(KT):
                    mm = nc.tensor.transpose(o_bank[:, k * L:(k + 1) * L], attn[:, k * P:(k + 1) * P], identf[:])
                mm.then_inc(attnT_ready, 1)

            def project_out(u, layer):
                need(pe, attnT_copied, u + 1)
                if isinstance(u, int) and u == 0:
                    pe.wait_ge(later_weights_loaded, 32)
                need(pe, maxT_step, MAXT_STEPS * upto(u + 2) + 2)
                if isinstance(u, int):
                    need(pe, norm_step, NORM_STEPS * (u - 1) + 1)
                for k in range(KT):
                    mm = nc.tensor.matmul(misc_bank[:, 0:D], attnT[:, k], wo_sb[:, layer, k],
                                          start=(k == 0), stop=(k == KT - 1))
                mm.then_inc(proj_ready, 1)

            def transpose_y(u, ru, layer):
                need(pe, affine_step, 2 * (u + 1))
                need(pe, qk_read, total(u + 7, *QK_READS, layer))
                for k in range(KT):
                    mm = nc.tensor.transpose(qk_bank[:, k * L:(k + 1) * L], y[:, ru % 2, k * P:(k + 1) * P], identf[:])
                mm.then_inc(yT_ready, 1)

            def phase(turn, step, loop_layer, masked):
                t, r = turn + step, step % RING
                r1, r2 = (r - 1) % RING, (r - 2) % RING
                if isinstance(t, int) and t == 0:
                    pe.wait_ge(k_padded, 1)
                now, before, last = live(t), live(t - 1), live(t - 2)
                ahead, ra, (layer_ahead, b_ahead) = live(t + 2), (r + 2) % RING, place(t + 2, loop_layer)
                if now:
                    scores(t, r, 0, masked)
                if last:
                    scoresT(t - 2, r2, 4, masked)
                if ahead:
                    project_qk(t + 2, ra, layer_ahead, b_ahead)
                if before:
                    transpose_max(t - 1, r1, loop_layer)
                if now:
                    scores(t, r, 1, masked)
                if last:
                    scoresT(t - 2, r2, 5, masked)
                if live(t - 3):
                    transpose_attn(t - 3)
                if last:
                    probs_v(t - 2, r2, 0)
                if now:
                    scores(t, r, 2, masked)
                if last:
                    scoresT(t - 2, r2, 6, masked)
                if live(t - 3):
                    project_out(t - 3, place(t - 3, loop_layer)[0])
                if now:
                    scores(t, r, 3, masked)
                if last:
                    scoresT(t - 2, r2, 7, masked)
                    transpose_o(t - 2, 0)
                if live(t - 4) and place(t - 4, loop_layer)[0] == 0:
                    transpose_y(t - 4, r, loop_layer)
                if now:
                    scores(t, r, 4, masked)
                if before:
                    scoresT(t - 1, r1, 0, masked)
                if ahead and layer_ahead == 0:
                    project_v(t + 2, ra)
                if now:
                    scores(t, r, 5, masked)
                if before:
                    scoresT(t - 1, r1, 1, masked)
                if last:
                    probs_v(t - 2, r2, 1)
                if now:
                    scores(t, r, 6, masked)
                if before:
                    scoresT(t - 1, r1, 2, masked)
                if now:
                    scores(t, r, 7, masked)
                if before:
                    scoresT(t - 1, r1, 3, masked)
                if last:
                    transpose_o(t - 2, 1)

            pe.wait_ge(ident_step, 6)
            for t in range(FIRST_PHASE, 0):
                phase(0, t, None, False)
            pe.wait_ge(flag_ready, 1)
            any_mask = pe.value_load(mask_flag[0:1, 0:1])
            with pe.If(any_mask):
                walk(pe, lambda turn, step, layer: phase(turn, step, layer, True), 0)
            with pe.Else():
                walk(pe, lambda turn, step, layer: phase(turn, step, layer, False), 0)


def kernel(**inputs):
    import concourse.bacc as bacc
    from concourse.bass_utils import run_bass_kernel_spmd

    def both(name):
        return [np.asarray(inputs[f"L{n}_xattn_{name}"]) for n in range(LAYERS)]

    q_order = np.arange(D).reshape(HEADS // 2, 2, HD).transpose(1, 2, 0).reshape(-1)
    k_order = np.arange(KVD).reshape(KV, HD).T.reshape(-1)
    o_order = np.arange(D).reshape(2, HALF, GROUP, HD).transpose(0, 2, 1, 3).reshape(-1)
    x, context = np.asarray(inputs["x"]), np.asarray(inputs["ctx_2048"])
    arrays = {
        "x": x,
        "xT": x.transpose(2, 0, 1),
        "ctxT": context.transpose(0, 2, 1),
        "mask": np.asarray(inputs["mask_Bx1xSxS2_ff0"]),
        "w_q": np.stack([w[:, q_order] for w in both("Wq")]),
        "w_kv": np.concatenate([w[:, k_order] for w in both("Wk")] + both("Wv"), axis=1),
        "w_o": np.stack([w[o_order] for w in both("Wo")]),
        "b_q": np.stack([b[q_order].reshape(KT, P) for b in both("bq")]).transpose(2, 0, 1),
        "b_k": np.concatenate([b[k_order] for b in both("bk")])[:, None],
        "rows": np.stack([np.concatenate(r) for r in zip(both("bo"), both("gamma"), both("beta"), both("bv"))]),
    }
    arrays["rows"] = arrays["rows"].reshape(-1)
    nc = bacc.Bacc("TRN2", target_bir_lowering=False, num_devices=1)
    arrays = {name: np.ascontiguousarray(a) for name, a in arrays.items()}
    args = [nc.dram_tensor(name, a.shape, mybir.dt.from_np(a.dtype), kind="ExternalInput").ap()
            for name, a in arrays.items()]
    result = nc.dram_tensor("result", (BATCH, L, D), F32, kind="ExternalOutput").ap()
    cross_attention(nc, *args, result)
    done = run_bass_kernel_spmd(nc, [arrays], core_ids=[0])
    return done.results[0]["result"]
```
